# Optimizing a Trainium2 kernel written in Bass

```python
import numpy as np
import jax
import jax.numpy as jnp

def _softmax(x, axis=-1):
    return jax.nn.softmax(x, axis=axis)

def _gelu(x):
    return jax.nn.gelu(x, approximate=True)

def _silu(x):
    return jax.nn.silu(x)

def _sigmoid(x):
    return jax.nn.sigmoid(x)

def _layernorm(x, axis=-1, eps=1e-05):
    m = jnp.mean(x, axis=axis, keepdims=True)
    v = jnp.var(x, axis=axis, keepdims=True)
    return (x - m) / jnp.sqrt(v + eps)

def _scatter_add(tgt, idx, src, axis=0):
    return tgt.at[idx].add(src)

def _segment_sum(src, seg, n):
    return jax.ops.segment_sum(src, seg, n)
kernel_name = 'mk_xattn_ffn_d1_seqx_r8_7f13d6'

def setup_inputs(seed: int=0):
    np.random.seed(seed)
    _w = jnp.asarray

    def _rec_inputs():
        import jax
        import jax.numpy as jnp
        _rk = jax.random.key(seed)
        x = -0.0002928 + 1 * jax.random.normal(jax.random.fold_in(_rk, 1), (8, 256, 256), jnp.float32)
        _lenS = 256 - jax.random.randint(jax.random.fold_in(_rk, 7), (8,), 0, max(1, 256 // 4) + 1, jnp.int32)
        _lenS2 = 1601 - jax.random.randint(jax.random.fold_in(_rk, 8), (8,), 0, max(1, 1601 // 4) + 1, jnp.int32)
        _ctx_512P = jax.random.normal(jax.random.fold_in(_rk, 11), (8, 16, 64), jnp.float32)
        _ctx_512c = jax.random.dirichlet(jax.random.fold_in(_rk, 511), 0.3 * jnp.ones((16,), jnp.float32), (8, 1601))
        _ctx_512t = jnp.einsum('bsk,bkd->bsd', _ctx_512c, _ctx_512P)
        _ctx_512t = _ctx_512t * jax.lax.rsqrt(jnp.mean(jnp.square(_ctx_512t)) + 1e-12) * 0.953939
        ctx_512 = 0.000227908 + 0.99994 * (_ctx_512t + 0.3 * jax.random.normal(jax.random.fold_in(_rk, 611), (8, 1601, 64), jnp.float32))
        return (x, ctx_512)
    x, ctx_512 = _rec_inputs()

    def _L0_xattn_setup():
        import jax, jax.numpy as jnp
        import numpy as np
        B, S, L = (2, 128, 128)
        DIM_Q, H, K, D_C, D_CQ, R = (256, 16, 128, 64, 192, 64)

        def _rope_tables(seq_len, dim, dtype):
            inv_freq = 1.0 / 10000.0 ** (jnp.arange(0, dim, 2, dtype=dtype) / dim)
            t = jnp.arange(seq_len, dtype=dtype)
            freqs = t[:, None] * inv_freq[None, :]
            sin = jnp.repeat(jnp.sin(freqs), 2, axis=-1)
            cos = jnp.repeat(jnp.cos(freqs), 2, axis=-1)
            return (sin, cos)

        def _rotate_half(x):
            h = x.shape[-1] // 2
            return jnp.concatenate([-x[..., h:], x[..., :h]], axis=-1)
        key = jax.random.key(seed)
        ks = jax.random.split(key, 8)
        s_in = 1.0 / np.sqrt(DIM_Q)
        s_k = 1.0 / np.sqrt(K)
        s_cq = 1.0 / np.sqrt(D_CQ)
        s_c = 1.0 / np.sqrt(D_C)
        return {'hidden_q': jax.random.normal(ks[0], (B, S, DIM_Q), jnp.float32), 'kv_c': jax.random.normal(ks[1], (B, L, D_C), jnp.float32), 'Wq': jax.random.normal(ks[2], (H * K, DIM_Q), jnp.float32) * s_in, 'w_kc_q': jax.random.normal(ks[3], (H, K, D_CQ), jnp.float32) * s_k, 'w_kc_kv': jax.random.normal(ks[4], (H, K, D_C), jnp.float32) * s_k, 'W_qr': jax.random.normal(ks[5], (H, D_CQ, R), jnp.float32) * s_cq / np.sqrt(R), 'W_kr': jax.random.normal(ks[6], (H, D_C, R), jnp.float32) * s_c, 'Wo': jax.random.normal(ks[7], (DIM_Q, H * K), jnp.float32) * s_k}
    _L0_xattn_all = _L0_xattn_setup()
    _L0_xattn_in = {k: v for k, v in _L0_xattn_all.items() if k in ('Wq', 'w_kc_q', 'w_kc_kv', 'W_qr', 'W_kr', 'Wo')}
    del _L0_xattn_all

    def _L0_ffn_setup():
        import jax, jax.numpy as jnp
        import numpy as np
        EPS = 1e-06
        K_STEPS = 4
        USE_GATING = True

        def layer_norm(x, gamma, beta):
            mu = jnp.mean(x, axis=-1, keepdims=True)
            var = jnp.mean(jnp.square(x - mu), axis=-1, keepdims=True)
            return (x - mu) * jax.lax.rsqrt(var + EPS) * gamma + beta
        key = jax.random.key(seed)
        B, L, D, H = (4, 512, 256, 1024)
        ks = jax.random.split(key, 16)
        s = 0.02
        return {'x': jax.random.normal(ks[0], (B, L, D), dtype=jnp.float32), 'in_gamma': jnp.ones((D,), jnp.float32), 'in_beta': jnp.zeros((D,), jnp.float32), 'agg_w': jax.random.normal(ks[1], (D, D), jnp.float32) * s, 'agg_b': jnp.zeros((D,), jnp.float32), 'pn_gamma': jnp.ones((D,), jnp.float32), 'pn_beta': jnp.zeros((D,), jnp.float32), 'd1_w': jax.random.normal(ks[2], (D, H), jnp.float32) * s, 'd1_b': jnp.zeros((H,), jnp.float32), 'd2_w': jax.random.normal(ks[3], (H, D), jnp.float32) * s, 'd2_b': jnp.zeros((D,), jnp.float32), 'bc_w': jax.random.normal(ks[4], (D, D), jnp.float32) * s, 'bc_b': jnp.zeros((D,), jnp.float32), 'gate_w': jax.random.normal(ks[5], (D, D), jnp.float32) * s, 'gate_b': jnp.zeros((D,), jnp.float32), 'out_gamma': jnp.ones((D,), jnp.float32), 'out_beta': jnp.zeros((D,), jnp.float32)}
    _L0_ffn_all = _L0_ffn_setup()
    _L0_ffn_in = {k: v for k, v in _L0_ffn_all.items() if k in ('in_gamma', 'in_beta', 'agg_w', 'agg_b', 'pn_gamma', 'pn_beta', 'd1_w', 'd1_b', 'd2_w', 'd2_b', 'bc_w', 'bc_b', 'gate_w', 'gate_b', 'out_gamma', 'out_beta')}
    del _L0_ffn_all
    return {'x': x, 'ctx_512': ctx_512, 'L0_xattn_Wq': _L0_xattn_in['Wq'], 'L0_xattn_w_kc_q': _L0_xattn_in['w_kc_q'], 'L0_xattn_w_kc_kv': _L0_xattn_in['w_kc_kv'], 'L0_xattn_W_qr': _L0_xattn_in['W_qr'], 'L0_xattn_W_kr': _L0_xattn_in['W_kr'], 'L0_xattn_Wo': _L0_xattn_in['Wo'], 'L0_ffn_in_gamma': _L0_ffn_in['in_gamma'], 'L0_ffn_in_beta': _L0_ffn_in['in_beta'], 'L0_ffn_agg_w': _L0_ffn_in['agg_w'], 'L0_ffn_agg_b': _L0_ffn_in['agg_b'], 'L0_ffn_pn_gamma': _L0_ffn_in['pn_gamma'], 'L0_ffn_pn_beta': _L0_ffn_in['pn_beta'], 'L0_ffn_d1_w': _L0_ffn_in['d1_w'], 'L0_ffn_d1_b': _L0_ffn_in['d1_b'], 'L0_ffn_d2_w': _L0_ffn_in['d2_w'], 'L0_ffn_d2_b': _L0_ffn_in['d2_b'], 'L0_ffn_bc_w': _L0_ffn_in['bc_w'], 'L0_ffn_bc_b': _L0_ffn_in['bc_b'], 'L0_ffn_gate_w': _L0_ffn_in['gate_w'], 'L0_ffn_gate_b': _L0_ffn_in['gate_b'], 'L0_ffn_out_gamma': _L0_ffn_in['out_gamma'], 'L0_ffn_out_beta': _L0_ffn_in['out_beta']}

def reference(x, ctx_512, L0_xattn_Wq, L0_xattn_w_kc_q, L0_xattn_w_kc_kv, L0_xattn_W_qr, L0_xattn_W_kr, L0_xattn_Wo, L0_ffn_in_gamma, L0_ffn_in_beta, L0_ffn_agg_w, L0_ffn_agg_b, L0_ffn_pn_gamma, L0_ffn_pn_beta, L0_ffn_d1_w, L0_ffn_d1_b, L0_ffn_d2_w, L0_ffn_d2_b, L0_ffn_bc_w, L0_ffn_bc_b, L0_ffn_gate_w, L0_ffn_gate_b, L0_ffn_out_gamma, L0_ffn_out_beta):
    import jax
    import jax.numpy as jnp

    def _L0_xattn_ref(hidden_q, kv_c, Wq, w_kc_q, w_kc_kv, W_qr, W_kr, Wo):
        import jax, jax.numpy as jnp
        import numpy as np
        B, S, L = (2, 128, 128)
        DIM_Q, H, K, D_C, D_CQ, R = (256, 16, 128, 64, 192, 64)

        def _rope_tables(seq_len, dim, dtype):
            inv_freq = 1.0 / 10000.0 ** (jnp.arange(0, dim, 2, dtype=dtype) / dim)
            t = jnp.arange(seq_len, dtype=dtype)
            freqs = t[:, None] * inv_freq[None, :]
            sin = jnp.repeat(jnp.sin(freqs), 2, axis=-1)
            cos = jnp.repeat(jnp.cos(freqs), 2, axis=-1)
            return (sin, cos)

        def _rotate_half(x):
            h = x.shape[-1] // 2
            return jnp.concatenate([-x[..., h:], x[..., :h]], axis=-1)
        b, s, _ = hidden_q.shape
        l = kv_c.shape[1]
        q_hk = (hidden_q @ Wq.T).reshape(b, s, H, K)
        q_big = jnp.einsum('bshk,hkq->bshq', q_hk, w_kc_q)
        sin, cos = _rope_tables(l, D_C, kv_c.dtype)
        kv_rope = kv_c * cos[None] + _rotate_half(kv_c) * sin[None]
        q_r = jnp.einsum('bshq,hqr->bhsr', q_big, W_qr)
        k_r = jnp.einsum('bld,hdr->bhlr', kv_rope, W_kr)
        scores = jnp.einsum('bhsr,bhlr->bhsl', q_r, k_r)
        attn = jax.nn.softmax(scores, axis=-1)
        ctx_c = jnp.einsum('bhsl,bld->bhsd', attn, kv_rope)
        ctx_lat = jnp.einsum('bhsd,hkd->bshk', ctx_c, w_kc_kv)
        out = ctx_lat.reshape(b, s, H * K) @ Wo.T
        return out

    def _L0_ffn_ref(x, in_gamma, in_beta, agg_w, agg_b, pn_gamma, pn_beta, d1_w, d1_b, d2_w, d2_b, bc_w, bc_b, gate_w, gate_b, out_gamma, out_beta):
        import jax, jax.numpy as jnp
        import numpy as np
        EPS = 1e-06
        K_STEPS = 4
        USE_GATING = True

        def layer_norm(x, gamma, beta):
            mu = jnp.mean(x, axis=-1, keepdims=True)
            var = jnp.mean(jnp.square(x - mu), axis=-1, keepdims=True)
            return (x - mu) * jax.lax.rsqrt(var + EPS) * gamma + beta
        x_norm = layer_norm(x, in_gamma, in_beta)
        thought = x_norm[:, -1, :] @ agg_w + agg_b
        for _ in range(K_STEPS):
            t = layer_norm(thought, pn_gamma, pn_beta)
            t = jax.nn.gelu(t @ d1_w + d1_b, approximate=False)
            thought = thought + (t @ d2_w + d2_b)
        broadcast = (thought @ bc_w + bc_b)[:, None, :]
        if USE_GATING:
            gate = jax.nn.sigmoid(x @ gate_w + gate_b)
            out = x + gate * broadcast
        else:
            out = x + broadcast
        return layer_norm(out, out_gamma, out_beta)
    x = x + _L0_xattn_ref(_layernorm(x, axis=-1), ctx_512, L0_xattn_Wq, L0_xattn_w_kc_q, L0_xattn_w_kc_kv, L0_xattn_W_qr, L0_xattn_W_kr, L0_xattn_Wo)
    x = x + _L0_ffn_ref(_layernorm(x, axis=-1), L0_ffn_in_gamma, L0_ffn_in_beta, L0_ffn_agg_w, L0_ffn_agg_b, L0_ffn_pn_gamma, L0_ffn_pn_beta, L0_ffn_d1_w, L0_ffn_d1_b, L0_ffn_d2_w, L0_ffn_d2_b, L0_ffn_bc_w, L0_ffn_bc_b, L0_ffn_gate_w, L0_ffn_gate_b, L0_ffn_out_gamma, L0_ffn_out_beta)
    return x

_drawn_inputs = setup_inputs


def setup_inputs(seed=0):
    import zlib

    import numpy as np

    out = dict(_drawn_inputs(seed))
    spreads = {'L0_ffn_in_gamma': (1.0, 0.6),
     'L0_ffn_in_beta': (0.0, 2.0),
     'L0_ffn_agg_b': (0.0, 0.67),
     'L0_ffn_pn_gamma': (1.0, 0.6),
     'L0_ffn_pn_beta': (0.0, 0.8),
     'L0_ffn_d1_b': (0.0, 0.8),
     'L0_ffn_d2_b': (0.0, 0.282),
     'L0_ffn_bc_b': (0.0, 0.381),
     'L0_ffn_gate_b': (0.0, 0.8),
     'L0_ffn_out_gamma': (1.0, 0.2),
     'L0_ffn_out_beta': (0.0, 0.1)}
    factors = {'L0_ffn_gate_w': 7.04}
    for name, (base, spread) in spreads.items():
        noise = np.random.default_rng([zlib.crc32(name.encode()), seed]).standard_normal(out[name].shape)
        drawn = base * np.exp(spread * noise) if base else spread * noise
        out[name] = jnp.asarray(drawn.astype(out[name].dtype))
    for name, factor in factors.items():
        out[name] = (out[name] * factor).astype(out[name].dtype)
    return out
```

```python
from contextlib import ExitStack

import numpy as np

import concourse.bass as bass
from concourse import mybir

F32 = mybir.dt.float32
F16 = mybir.dt.float16
BF16 = mybir.dt.bfloat16
ALU = mybir.AluOpType
ACT = mybir.ActivationFunctionType
AX = mybir.AxisListType

FFN_DMAS = 15
B, S, DM = 8, 256, 256
L, DC = 1601, 64
H, DK, DCQ, DR = 16, 128, 192, 64
HID = 1024
K_STEPS = 4
NP = H // 2
QW = 2 * S
KT = 13
LAST = L - 128 * (KT - 1)
LP = 128 * KT
ST = S // 128
SC = 16.0
LAG = 5
HALF = (801, 800)
POOL_TILES = 7
POOL_OPS = POOL_TILES - 1
DVE_OPS = KT - POOL_TILES
LN_OPS = 8
PREP_OPS = 11
RAW_DMAS = 8
POST_OPS = 13


def build_xattn_ffn(nc, x, kv, kvt, cos_t, sin_t, cos_n, sin_n, ident_in, sel_in, wq, wkcq_t, wkckv, wqr_t, wkr_t, wo_t,
                    in_gamma, in_beta, agg_w, agg_b, pn_gamma, pn_beta, d1_w, d1_b, d2_w, d2_b,
                    bc_w, bc_b, gate_w, gate_b, out_gamma, out_beta, out):
    with ExitStack() as ctx:
        def sb(name, shape, dt=F32):
            return ctx.enter_context(nc.sbuf_tensor(name, shape, dt))

        def sem(name):
            return ctx.enter_context(nc.semaphore(name))

        xs = sb("xs", [128, B * ST * DM])
        xnt = sb("xnt", [128, 2 * B * S])
        mw = sb("mw", [128, 2, H * DC])
        nw = sb("nw", [128, NP, DM])
        cost = sb("cost", [128, L])
        sint = sb("sint", [128, L])
        cosn = sb("cosn", [128, KT * DC])
        sinn = sb("sinn", [128, KT * DC])
        raw_t = sb("raw_t", [128, L])
        rot_t = sb("rot_t", [128, L])
        raw_n = sb("raw_n", [128, KT, DC])
        rot_n = sb("rot_n", [128, KT, DC])
        k_hi = [sb(f"k_hi{i}", [128, LP], F16) for i in range(2)]
        k_lo = [sb(f"k_lo{i}", [96, LP], F16) for i in range(2)]
        k_n = [sb(f"k_n{i}", [128, KT, DC]) for i in range(2)]
        qq = [sb(f"qq{i}", [128, 2, QW], F16) for i in range(4)]
        q_hi = [sb(f"q_hi{i}", [128, S], F16) for i in range(2)]
        q_lo = [sb(f"q_lo{i}", [128, S], F16) for i in range(2)]
        big = sb("big", [128, 12 * QW + 2 * NP * S + B * ST * DM])
        pr = big[:, 0:12 * QW].rearrange("p (t q) -> p t q", t=12)
        pr_last = sb("pr_last", [128, QW])
        ctx_n = [big[:, 12 * QW + i * NP * S:12 * QW + (i + 1) * NP * S].rearrange("p (g q) -> p g q", g=NP)
                 for i in range(2)]
        gates = big[:, 12 * QW + 2 * NP * S:12 * QW + 2 * NP * S + B * ST * DM]
        acc_p = [sb(f"acc_p{i}", [128, QW]) for i in range(2)]
        acc_d = sb("acc_d", [128, QW])
        rinv = sb("rinv", [128, S])
        mx = sb("mx", [128, 8])
        negm = sb("negm", [128, 4], BF16)
        ident = sb("ident", [128, 128])
        identb = sb("identb", [128, 128], BF16)
        ones = sb("ones", [128, DC])
        u = sb("u", [128, ST, DM])
        ut = sb("ut", [128, 2, S])
        gw = sb("gw", [128, 2, DM])
        gb = sb("gb", [128, DM])
        stats = sb("stats", [128, ST, 6])
        mv = sb("mv", [128, ST, 2])
        ve = sb("ve", [128, ST])
        sd = sb("sd", [128, ST])
        rs = sb("rs", [128, ST])

        z = sb("z", [128, ST, DM])
        mean_all = sb("mean_all", [128, B * ST])
        rs_all = sb("rs_all", [128, B * ST])
        a2 = sb("a2", [DCQ - 128, H, DC])
        bw = sb("bw", [128, H, DC])
        xn = [ut, u]

        cut = np.cumsum([0, H * DM, H * DK, H * DK, H * DM, H * DC, H * DC])
        assert cut[-1] <= big.shape[1] and H * (DCQ + DC) <= xnt.shape[1]
        wqs, wkcq1, wkcq2, wos, wkckvs, a1 = (
            big[:, int(cut[i]):int(cut[i + 1])].rearrange("p (h c) -> p h c", h=H) for i in range(6))
        wqr = xnt[0:DR, 0:H * DCQ].rearrange("p (h q) -> p h q", h=H)
        wkr = xnt[0:DR, H * DCQ:H * (DCQ + DC)].rearrange("p (h d) -> p h d", h=H)

        d1s = xnt[:, 0:2 * HID].rearrange("p (t h) -> p t h", t=2)
        d2s = xnt[:, 2 * HID:4 * HID].rearrange("p (t m) -> p t m", t=HID // 128)
        aggs = cost[:, 0:2 * DM].rearrange("p (t m) -> p t m", t=2)
        bcs = cost[:, 2 * DM:4 * DM].rearrange("p (t m) -> p t m", t=2)
        ogs, obs = cost[:, 4 * DM:5 * DM], cost[:, 5 * DM:6 * DM]
        ig8, ib8, pg8, pb8, ab8, db8 = (sint[0:B, i * DM:(i + 1) * DM] for i in range(6))
        bb8 = raw_t[0:B, 0:DM]
        d1bs = raw_t[:, DM:DM + HID // 128]
        sels = rot_t[0:B, 0:B * 128].rearrange("p (b q) -> p b q", b=B)
        u_all = big[:, 0:B * ST * DM]
        th = sb("th", [B, DM])
        v8 = sb("v8", [B, DM])
        w8 = sb("w8", [B, DM])
        tt = sb("tt", [128, 2, B])
        hp = sb("hp", [128, HID // 128, B])
        ht = sb("ht", [128, HID // 128, B])
        st8, mv8, ve8, sd8, rs8 = sb("st8", [B, 6]), sb("mv8", [B, 2]), sb("ve8", [B, 1]), sb("sd8", [B, 1]), sb("rs8", [B, 1])
        st_f = sb("st_f", [128, B * ST, 6])
        mv_f = sb("mv_f", [128, B * ST, 2])
        ve_f, sd_f, rs_f, nm_f = (sb(k, [128, B * ST]) for k in ("ve_f", "sd_f", "rs_f", "nm_f"))

        ps_m = ctx.enter_context(nc.psum_tensor("ps_m", [128, 2, 1024], F32))
        ps_s = ctx.enter_context(nc.psum_tensor("ps_s", [128, 2, 512], F32))
        ps_o = ctx.enter_context(nc.psum_tensor("ps_o", [128, 512], F32))
        ps_x = ctx.enter_context(nc.psum_tensor("ps_x", [128, 512], F32))

        in_x, in_wa, in_wb, in_wc, in_tab, in_raw = (sem(s) for s in ("in_x", "in_wa", "in_wb", "in_wc", "in_tab", "in_raw"))
        in_gate, in_ffn, in_row = sem("in_gate"), sem("in_ffn"), sem("in_row")
        dve_const, ln = sem("dve_const"), sem("ln")
        const_done = sem("const_done")
        wfold, wcopy = sem("wfold"), sem("wcopy")
        xt_done, xt_copied, ln_sd = sem("xt_done"), sem("xt_copied"), sem("ln_sd")
        prep = sem("prep")
        q_done, qh_done, ql_done = sem("q_done"), sem("qh_done"), sem("ql_done")
        in_qq = [sem("in_qq0"), sem("in_qq1")]
        mx_done, mx_read, negm_done = sem("mx_done"), sem("mx_read"), sem("negm_done")
        mrow_done, mrow_copied = sem("mrow_done"), sem("mrow_copied")
        st_done, p_done, pv_done = sem("st_done"), sem("p_done"), sem("pv_done")
        sum_p, sum_d = sem("sum_p"), sem("sum_d")
        total_done, rinv_done, ctx_done = sem("total_done"), sem("rinv_done"), sem("ctx_done")
        proj_done, post, sd_done = sem("proj_done"), sem("post"), sem("sd_done")
        ut_done, ut_copied, gate_done, z_done, gate_out = (sem(s) for s in ("ut_done", "ut_copied", "gate_done", "z_done", "gate_out"))
        t_dve = sem("t_dve")
        var8, dev8, tr_in, tr8, trc8, lin8, pre8, gelu8 = (
            sem(s) for s in ("var8", "dev8", "tr_in", "tr8", "trc8", "lin8", "pre8", "gelu8"))
        u_ready, xb_ready, spread, mixed, added, var_f, dev_f, coef_f, normed, scaled, final, stored = (
            sem(s) for s in ("u_ready", "xb_ready", "spread", "mixed", "added", "var_f", "dev_f", "coef_f", "normed", "scaled",
                             "final", "stored"))

        block = ctx.enter_context(nc.Block())

        def key_cols(t):
            return slice(128 * t, 128 * t + (128 if t < KT - 1 else LAST))

        def probs(t):
            return pr[:, t, :] if t < KT - 1 else pr_last[:, :]

        def batches(eng, batch):
            batch(0, 0)
            with eng.Fori(0, (B - 2) // 2) as i:
                batch(i * 2 + 1, 1)
                batch(i * 2 + 2, 0)
            batch(B - 1, 1)

        def first(n):
            return isinstance(n, int) and n == 0

        def last(n):
            return isinstance(n, int) and n == B - 1

        @block.sync
        def _(sp):
            sp.dma_start(wqr, wqr_t.rearrange("h r q -> r h q")).then_inc(in_wa, 16)
            sp.dma_start(wkr, wkr_t.rearrange("h r d -> r h d")).then_inc(in_wa, 16)
            sp.dma_start(xs[:, :].rearrange("p (b s m) -> p b s m", b=B, s=ST),
                         x.rearrange("b (s p) m -> p b s m", p=128)).then_inc(in_x, 16)

            def load_keys(n):
                for h in range(2):
                    sp.dma_start(raw_t[64 * h:64 * h + 64, :], kvt[n, :, :]).then_inc(in_raw, 16)
                    sp.dma_start(rot_t[64 * h:64 * h + 32, :], kvt[n, 32:64, :]).then_inc(in_raw, 16)
                    sp.dma_start(rot_t[64 * h + 32:64 * h + 64, :], kvt[n, 0:32, :]).then_inc(in_raw, 16)
                sp.dma_start(raw_n[:, 0:KT - 1, :], kv[n, 0:128 * (KT - 1), :].rearrange("(t p) d -> p t d", p=128)).then_inc(in_raw, 16)
                sp.dma_start(raw_n[0:LAST, KT - 1, :], kv[n, 128 * (KT - 1):L, :]).then_inc(in_raw, 16)

            sp.wait_ge(const_done, 1)
            load_keys(0)
            for dst, src in ((cost, cos_t), (sint, sin_t)):
                for h in range(2):
                    sp.dma_start(dst[64 * h:64 * h + 64, :], src).then_inc(in_tab, 16)
            sp.dma_start(cosn[:, :], cos_n).then_inc(in_tab, 16)
            sp.dma_start(sinn[:, :], sin_n).then_inc(in_tab, 16)

            def move_queries(p, g):
                sp.wait_ge(qh_done, g + 1)
                sp.wait_ge(ql_done, g + 1)
                if not (isinstance(g, int) and g < 4):
                    sp.wait_ge(st_done, g * KT - 3 * KT)
                d, r = qq[p % 4], p % 2
                for h in range(2):
                    for j in range(2):
                        sp.dma_start(d[0:64, j, h * S:(h + 1) * S], q_hi[r][64 * h:64 * h + 64, :]).then_inc(in_qq[r], 16)
                    sp.dma_start(d[64:128, 0, h * S:(h + 1) * S], q_lo[r][64 * h:64 * h + 64, :]).then_inc(in_qq[r], 16)

            sp.wait_ge(const_done, 4)
            move_queries(0, 0)
            move_queries(1, 1)

            def batch(n, par):
                if not last(n):
                    sp.wait_ge(prep, (n + 1) * PREP_OPS)
                    load_keys(n + 1)
                for p in range(NP - 2 if last(n) else NP):
                    move_queries((p + 2) % NP, n * NP + p + 2)

            batches(sp, batch)
            sp.wait_ge(q_done, B * NP)
            sp.wait_ge(prep, B * PREP_OPS)
            for dst, src in ((d1s, d1_w), (d2s, d2_w), (aggs, agg_w), (bcs, bc_w)):
                sp.dma_start(dst, src.rearrange("(t p) m -> p t m", p=128)).then_inc(in_ffn, 16)
            for dst, src in ((ogs, out_gamma), (obs, out_beta)):
                sp.dma_start(dst, src.partition_broadcast(128)).then_inc(in_ffn, 16)
            for dst, src in ((ig8, in_gamma), (ib8, in_beta), (pg8, pn_gamma), (pb8, pn_beta), (ab8, agg_b), (db8, d2_b), (bb8, bc_b)):
                sp.dma_start(dst, src.partition_broadcast(B)).then_inc(in_ffn, 16)
            sp.dma_start(d1bs, d1_b).then_inc(in_ffn, 16)
            sp.dma_start(sels, sel_in).then_inc(in_ffn, 16)
            sp.wait_ge(post, (B - 1) * POST_OPS + 4)
            sp.dma_start(th[:, :], xs[127:128, :].rearrange("p (b s m) -> p b s m", b=B, s=ST)[:, :, ST - 1, :]).then_inc(in_row, 16)
            for b in range(B):
                sp.wait_ge(final, b + 1)
                sp.dma_start(out[b].rearrange("(s p) m -> p s m", p=128),
                             gates[:, b * ST * DM:(b + 1) * ST * DM].rearrange("p (s m) -> p s m", s=ST)).then_inc(stored, 16)
            sp.wait_ge(stored, 16 * B)

        @block.gpsimd
        def _(pool):
            pool.dma_start(gw[:, :, :], gate_w.rearrange("(t p) m -> p t m", p=128)).then_inc(in_gate, 16)
            pool.dma_start(gb[:, :], gate_b.partition_broadcast(128)).then_inc(in_gate, 16)

            def keys(n, par, k):
                def chained(ins):
                    ins.then_inc(prep, 1)
                    return ins
                if k == 0:
                    pool.wait_ge(in_raw, n * (16 * RAW_DMAS) + 16 * RAW_DMAS)
                    if first(n):
                        pool.wait_ge(in_tab, 16 * 6)
                else:
                    pool.wait_ge(prep, n * PREP_OPS + k)
                if k == 0:
                    chained(pool.tensor_tensor(raw_t[:, :], raw_t[:, :], cost[:, :], ALU.mult))
                elif k == 1:
                    chained(pool.tensor_tensor(rot_t[:, :], rot_t[:, :], sint[:, :], ALU.mult))
                elif k == 2:
                    chained(pool.tensor_tensor(k_hi[par][:, 0:L], raw_t[:, :], rot_t[:, :], ALU.add))
                elif k == 3:
                    chained(pool.tensor_tensor(raw_t[0:DC, :], raw_t[0:DC, :], rot_t[0:DC, :], ALU.add))
                elif k == 4:
                    chained(pool.tensor_tensor(k_lo[par][0:DC, 0:L], raw_t[0:DC, :], k_hi[par][0:DC, 0:L], ALU.subtract))
                elif k in (5, 6):
                    a = 32 * (k - 5)
                    chained(pool.tensor_tensor(rot_n[:, :, a:a + 32], raw_n[:, :, 32 - a:64 - a],
                                               sinn[:, :].rearrange("p (t d) -> p t d", t=KT)[:, :, a:a + 32], ALU.mult))
                elif k == 7:
                    chained(pool.tensor_tensor(raw_n[:, :, :], raw_n[:, :, :],
                                               cosn[:, :].rearrange("p (t d) -> p t d", t=KT), ALU.mult))
                elif k == 8:
                    chained(pool.tensor_tensor(k_n[par][:, 0:6, :], raw_n[:, 0:6, :], rot_n[:, 0:6, :], ALU.add))
                elif k == 9:
                    chained(pool.tensor_tensor(k_n[par][:, 6:12, :], raw_n[:, 6:12, :], rot_n[:, 6:12, :], ALU.add))
                elif k == 10:
                    chained(pool.tensor_tensor(k_n[par][:, 12, :], raw_n[:, 12, :], rot_n[:, 12, :], ALU.add))

            for k in range(PREP_OPS):
                keys(0, 0, k)

            when = {1: (0, 1), 2: (2,), 3: (3,), 4: (4, 5), 5: (6, 7), 6: (8, 9, 10)}

            def batch(n, par):
                for p in range(NP):
                    g = n * NP + p
                    for t in range(1, POOL_TILES):
                        if t == 1 and not (first(n) and p < 2):
                            pool.wait_ge(sum_d, g * DVE_OPS - DVE_OPS)
                        if t > 1:
                            pool.wait_ge(sum_p, g * POOL_OPS + t - 1)
                        pool.wait_ge(p_done, g * KT + t + 1)
                        a = probs(0) if t == 1 else acc_p[p % 2][:, :]
                        pool.tensor_tensor(acc_p[p % 2][:, :], a, probs(t), ALU.add).then_inc(sum_p, 1)
                    if not last(n):
                        if p == 1 and not first(n):
                            pool.wait_ge(st_done, n * (NP * KT))
                            pool.wait_ge(pv_done, n * (NP * KT))
                        for k in when.get(p, ()):
                            keys(n + 1, 1 - par, k)

            batches(pool, batch)
            pool.wait_ge(pv_done, B * NP * KT)
            pool.wait_ge(post, B * POST_OPS)
            pool.wait_ge(sum_d, B * NP * DVE_OPS)
            for i in range(B * ST):
                pool.tensor_scalar(u_all[:, i * DM:(i + 1) * DM], xs[:, i * DM:(i + 1) * DM], mean_all[:, i:i + 1],
                                   rs_all[:, i:i + 1], ALU.subtract, ALU.mult).then_inc(u_ready, 1)
            pool.wait_ge(u_ready, B * ST)
            pool.wait_ge(in_ffn, 16 * FFN_DMAS)
            pool.wait_ge(in_row, 16)
            for b in range(B):
                c = slice(b * ST * DM, (b + 1) * ST * DM)
                for i in range(ST):
                    d = slice(c.start + i * DM, c.start + (i + 1) * DM)
                    o = pool.tensor_tensor(xs[:, d], xs[:, d], obs, ALU.add)
                o.then_inc(xb_ready, 1)
            for b in range(B):
                c = slice(b * ST * DM, (b + 1) * ST * DM)
                pool.wait_ge(mixed, b + 1)
                pool.tensor_tensor(gates[:, c], gates[:, c], u_all[:, c], ALU.add).then_inc(added, 1)
            for b in range(B):
                c = slice(b * ST * DM, (b + 1) * ST * DM)
                pool.wait_ge(xb_ready, B)
                pool.wait_ge(scaled, b + 1)
                pool.tensor_tensor(gates[:, c], gates[:, c], xs[:, c], ALU.add).then_inc(final, 1)

        @block.scalar
        def _(act):
            act.dma_start(wkcq1, wkcq_t[:, 0:128, :].rearrange("h q k -> q h k")).then_inc(in_wb, 16)
            act.dma_start(wkcq2[0:64], wkcq_t[:, 128:DCQ, :].rearrange("h q k -> q h k")).then_inc(in_wb, 16)
            act.dma_start(wqs, wq.rearrange("(h k) m -> k h m", k=DK)).then_inc(in_wb, 16)
            act.dma_start(ident[:, :], ident_in).then_inc(in_wa, 16)
            act.dma_start(wos, wo_t.rearrange("(h k) m -> k h m", k=DK)).then_inc(in_wc, 16)
            act.dma_start(wkckvs, wkckv.rearrange("h k d -> k h d")).then_inc(in_wc, 16)

            def copy(out_, in_, **kw):
                return act.activation(out_, in_, ACT.Copy, **kw)

            act.wait_ge(wfold, 1)
            copy(a1[:, 0:8, :].rearrange("p h d -> p (h d)"), ps_m[:, 0, 0:512]).then_inc(wcopy, 1)
            act.wait_ge(wfold, 2)
            copy(a1[:, 8:16, :].rearrange("p h d -> p (h d)"), ps_m[:, 0, 512:1024]).then_inc(wcopy, 1)
            for i in range(2):
                act.wait_ge(wfold, 4 + i + 1)
                copy(bw[:, 8 * i:8 * i + 8, :].rearrange("p h d -> p (h d)"), ps_s[:, i, :]).then_inc(wcopy, 1)
            for i in range(4):
                act.wait_ge(wfold, 6 + i + 1)
                copy(mw[:, i // 2, (i % 2) * 512:(i % 2 + 1) * 512], ps_m[:, i // 2, (i % 2) * 512:(i % 2 + 1) * 512]).then_inc(wcopy, 1)
            for b in range(B):
                act.wait_ge(ln, LN_OPS * b + 5)
                act.activation(sd[:, :], ve[:, :], ACT.Sqrt).then_inc(ln_sd, 1)
                act.wait_ge(xt_done, b + 1)
                copy(xnt[:, :].rearrange("p (t q) -> p t q", t=2)[:, :, b * S:(b + 1) * S],
                     (ps_x if b % 2 else ps_o)[:, :].rearrange("p (t q) -> p t q", t=2)).then_inc(xt_copied, 1)

            def high_part(p, g):
                act.wait_ge(q_done, g + 1)
                copy(q_hi[p % 2][:, :], ps_x[:, 0:S], scale=SC).then_inc(qh_done, 1)

            def copy_row(p, g):
                act.wait_ge(mrow_done, g + 1)
                copy(qq[p % 4][64:65, 1, :], ps_x[64:65, :], scale=1.0 / SC).then_inc(mrow_copied, 1)

            act.wait_ge(const_done, 7)
            high_part(0, 0)
            high_part(1, 1)
            copy_row(0, 0)
            for i in range(4):
                act.wait_ge(wfold, 10 + i + 1)
                copy(nw[:, 2 * i:2 * i + 2, :].rearrange("p g m -> p (g m)"), ps_m[:, i // 2, (i % 2) * 512:(i % 2 + 1) * 512]).then_inc(wcopy, 1)

            def batch(n, par):
                for p in range(NP):
                    g = n * NP + p
                    for t in range(KT):
                        G = n * (NP * KT) + (p * KT + t)
                        act.wait_ge(st_done, G + 1)
                        if not (first(n) and p == 0):
                            act.wait_ge(pv_done, G + 1 - KT)
                            if t < POOL_TILES:
                                act.wait_ge(sum_p, g * POOL_OPS - POOL_OPS + max(t, 1))
                            else:
                                act.wait_ge(sum_d, g * DVE_OPS - DVE_OPS + max(t - POOL_TILES, 1))
                        r = 128 if t < KT - 1 else LAST
                        act.activation(probs(t)[0:r, :], ps_s[0:r, (p * KT + t) % 2, :], ACT.Exp, scale=1.0 / SC).then_inc(p_done, 1)
                        if t == 7 and not (last(n) and p >= NP - 2):
                            act.wait_ge(in_qq[p % 2], n * (96 * 4) + 96 * (p // 2 + 1))
                            high_part(p, g + 2)
                        if t == 10 and not (last(n) and p == NP - 1):
                            copy_row(p + 1, g + 1)
                        if not first(n):
                            if p == 2 and t == 6:
                                deviation(act, n - 1)
                            if p == 4 and t == 0:
                                copy_ut(act, n - 1)
                            if p == 6 and t == 2:
                                gate(act, n - 1)

            def deviation(act, m):
                act.wait_ge(post, m * POST_OPS + 7)
                act.activation(sd[:, :], ve[:, :], ACT.Sqrt).then_inc(sd_done, 1)

            def copy_ut(act, m):
                act.wait_ge(ut_done, m + 1)
                copy(ut[:, :, :], ps_x[:, :].rearrange("p (t q) -> p t q", t=2)).then_inc(ut_copied, 1)

            def gate(act, m):
                act.wait_ge(post, m * POST_OPS + 13)
                act.activation(gates[:, bass.ds(m * (ST * DM), ST * DM)], z[:, :, :].rearrange("p s m -> p (s m)"),
                               ACT.Sigmoid).then_inc(gate_out, 1)

            batches(act, batch)
            deviation(act, B - 1)
            copy_ut(act, B - 1)
            gate(act, B - 1)
            for k in range(2 + K_STEPS):
                act.wait_ge(var8, k + 1)
                act.activation(sd8[:, :], ve8[:, :], ACT.Sqrt).then_inc(dev8, 1)
                if k >= 2:
                    act.wait_ge(pre8, k - 1)
                    act.activation(ht[:, :, :], hp[:, :, :], ACT.Gelu).then_inc(gelu8, 1)
            act.wait_ge(var_f, 1)
            act.activation(sd_f[:, :], ve_f[:, :], ACT.Sqrt).then_inc(dev_f, 1)
            act.wait_ge(coef_f, 1)
            for i in range(B * ST):
                act.activation(gates[:, i * DM:(i + 1) * DM], gates[:, i * DM:(i + 1) * DM], ACT.Identity,
                               bias=nm_f[:, i:i + 1], scale=rs_f[:, i:i + 1]).then_inc(normed, 1)

        @block.tensor
        def _(pe):
            pe.wait_ge(in_wa, 48)
            for part, rows in ((0, 128), (1, 64)):
                for hg in range(2):
                    for h in range(8 * hg, 8 * hg + 8):
                        mm = pe.matmul(ps_m[0:rows, part, hg * 512 + (h % 8) * DC:hg * 512 + (h % 8 + 1) * DC],
                                       wqr[:, h, 128 * part:128 * part + rows], wkr[:, h, :], start=True, stop=True)
                    mm.then_inc(wfold, 1)
            pe.wait_ge(in_wb, 48)
            pe.wait_ge(wcopy, 4)
            for h in range(H):
                d = ps_s[:, h // 8, (h % 8) * DC:(h % 8 + 1) * DC]
                pe.matmul(d, wkcq1[:, h, :], a1[:, h, :], start=True, stop=False)
                mm = pe.matmul(d, wkcq2[0:64, h, :], a2[:, h, :], start=False, stop=True)
                if h % 8 == 7:
                    mm.then_inc(wfold, 1)
            pe.wait_ge(wcopy, 6)
            for mt in range(2):
                for h in range(H):
                    mm = pe.matmul(ps_m[:, mt, h * DC:(h + 1) * DC], wqs[:, h, 128 * mt:128 * mt + 128], bw[:, h, :],
                                   start=True, stop=True)
                    if h % 8 == 7:
                        mm.then_inc(wfold, 1)
            for b in range(B):
                pe.wait_ge(ln, LN_OPS * (b + 1))
                if b >= 2:
                    pe.wait_ge(xt_copied, b - 1)
                for mt in range(2):
                    for st in range(ST):
                        mm = pe.transpose((ps_x if b % 2 else ps_o)[:, mt * S + st * 128:mt * S + st * 128 + 128],
                                          xn[b % 2][:, st, 128 * mt:128 * mt + 128], ident[:, :])
                mm.then_inc(xt_done, 1)

            def queries(n, p, g):
                for mt in range(2):
                    mm = pe.matmul(ps_x[:, 0:S], mw[:, mt, p * 128:(p + 1) * 128],
                                   xnt[:, bass.ds(n * S + mt * B * S, S)],
                                   start=(mt == 0), stop=(mt == 1))
                mm.then_inc(q_done, 1)

            def max_half(par, p, g, i):
                a = (i // 2) * 128
                q = qq[p % 4][:, 0, a:a + 128]
                c = HALF[0] * (i % 2)
                pe.matmul(ps_m[:, i % 2, 0:512], q, k_hi[par][:, c:c + 512], start=True, stop=True)
                w = HALF[i % 2] - 512
                pe.matmul(ps_m[:, i % 2, 512:512 + w], q, k_hi[par][:, c + 512:c + 512 + w],
                          start=True, stop=True).then_inc(mx_done, 1)

            def max_row(g):
                pe.wait_ge(negm_done, g + 1)
                for i in range(4):
                    mm = pe.matmul(ps_x[64:65, i * 128:(i + 1) * 128], negm[:, i:i + 1], identb[:, :], start=True, stop=True)
                mm.then_inc(mrow_done, 1)

            pe.wait_ge(xt_copied, B)
            pe.wait_ge(wcopy, 10)
            queries(0, 0, 0)
            pe.wait_ge(ql_done, 1)
            queries(0, 1, 1)
            pe.wait_ge(prep, PREP_OPS)
            pe.wait_ge(in_qq[0], 96)
            for i in range(8):
                if i >= 2:
                    pe.wait_ge(mx_read, i - 1)
                max_half(0, 0, 0, i)
            pe.wait_ge(ql_done, 2)
            max_row(0)
            pe.wait_ge(mx_read, 8)
            pe.wait_ge(in_wc, 32)
            for p in range(NP):
                for h in range(2):
                    mm = pe.matmul(ps_m[64 * h:64 * h + 64, p // 4, (p % 4) * DM:(p % 4 + 1) * DM],
                                   wkckvs[:, 2 * p + h, :], wos[:, 2 * p + h, :], start=True, stop=True)
                if p % 2:
                    mm.then_inc(wfold, 1)
            pe.wait_ge(wcopy, 14)
            pe.wait_ge(const_done, 7)

            def p_kv(par, p, t, G):
                pe.wait_ge(p_done, G + 1)
                for h in range(2):
                    mm = pe.matmul(ps_o[64 * h:64 * h + 64, 0:S], k_n[par][:, t, :], probs(t)[:, h * S:(h + 1) * S],
                                   start=(t == 0), stop=(t == KT - 1))
                mm.then_inc(pv_done, 1)

            def totals(g):
                pe.wait_ge(sum_d, g * DVE_OPS + DVE_OPS)
                for h in range(2):
                    mm = pe.matmul(ps_x[64 * h:64 * h + 64, 0:S], ones[:, :], acc_d[:, h * S:(h + 1) * S], start=True, stop=True)
                mm.then_inc(total_done, 1)

            def project(par, m):
                pe.wait_ge(ctx_done, m * NP + NP)
                for st in range(ST):
                    for p in range(NP):
                        mm = pe.matmul(ps_x[:, st * DM:(st + 1) * DM], ctx_n[par][:, p, st * 128:st * 128 + 128], nw[:, p, :],
                                       start=(p == 0), stop=(p == NP - 1))
                mm.then_inc(proj_done, 1)

            def transpose_u(m):
                pe.wait_ge(post, m * POST_OPS + 10)
                for mt in range(2):
                    for st in range(ST):
                        mm = pe.transpose(ps_x[:, mt * S + st * 128:mt * S + st * 128 + 128], u[:, st, 128 * mt:128 * mt + 128],
                                          ident[:, :])
                mm.then_inc(ut_done, 1)

            def gate_mm(m):
                pe.wait_ge(ut_copied, m + 1)
                pe.wait_ge(in_gate, 32)
                for st in range(ST):
                    for mt in range(2):
                        mm = pe.matmul(ps_x[:, st * DM:(st + 1) * DM], ut[:, mt, st * 128:st * 128 + 128], gw[:, mt, :],
                                       start=(mt == 0), stop=(mt == 1))
                mm.then_inc(gate_done, 1)

            def batch(n, par):
                for p in range(NP):
                    g = n * NP + p
                    ahead = not (last(n) and p == NP - 1)
                    for t in range(KT):
                        j = p * KT + t
                        G = n * (NP * KT) + j
                        c = key_cols(t)
                        r = c.stop - c.start
                        if t == 0:
                            pe.wait_ge(mrow_copied, g + 1)
                        if not (first(n) and j < 2):
                            pe.wait_ge(p_done, G - 1)
                        pe.matmul(ps_s[0:r, j % 2, :], k_hi[par][:, c], qq[p % 4][:, 0, :], start=True, stop=False)
                        pe.matmul(ps_s[0:r, j % 2, :], k_lo[par][:, c], qq[p % 4][0:96, 1, :], start=False, stop=True).then_inc(st_done, 1)
                        if ahead and t < 8:
                            if t == 0:
                                pe.wait_ge(in_qq[(p + 1) % 2], n * (96 * 4) + 96 * ((p + 1) // 2 + 1))
                                if p == NP - 1:
                                    pe.wait_ge(prep, n * PREP_OPS + 2 * PREP_OPS)
                            pe.wait_ge(mx_read, g * 8 + (8 + t - 1))
                            max_half(par if p < NP - 1 else 1 - par, p + 1, g + 1, t)
                        if t == 2 and not (first(n) and p == 0):
                            if not first(n) and p in (2, 4, 6):
                                if p == 2:
                                    pe.wait_ge(post, (n - 1) * POST_OPS + 4)
                                elif p == 4:
                                    pe.wait_ge(ut_copied, n)
                                else:
                                    pe.wait_ge(post, (n - 1) * POST_OPS + 13)
                            else:
                                pe.wait_ge(mrow_copied, g + 1)
                            totals(g - 1)
                        if t == 6 and not (last(n) and p >= NP - 2):
                            if not (first(n) and p == 0):
                                pe.wait_ge(rinv_done, g)
                            queries(n if p < NP - 2 else n + 1, (p + 2) % NP, g + 2)
                        if t == 9 and ahead:
                            if last(n) and p == NP - 2:
                                pe.wait_ge(rinv_done, g)
                            else:
                                pe.wait_ge(ql_done, g + 3)
                            max_row(g + 1)
                        if t == 11 and not first(n) and p in (1, 3, 5):
                            pe.wait_ge(mrow_copied, g + 2)
                            if p == 1:
                                project(1 - par, n - 1)
                            elif p == 3:
                                transpose_u(n - 1)
                            else:
                                gate_mm(n - 1)
                        tt, back = t - LAG, 0
                        if tt < 0:
                            tt, back = tt + KT, 1
                        if first(n) and p == 0 and back:
                            continue
                        if tt == 0 and not (first(n) and p == 0):
                            pe.wait_ge(ctx_done, g)
                        p_kv(1 - par if back and p == 0 else par, p - back, tt, G - LAG)

            batches(pe, batch)
            G = B * NP * KT
            for t in range(KT - LAG, KT):
                p_kv(1, NP - 1, t, G - KT + t)
            totals(B * NP - 1)
            pe.wait_ge(rinv_done, B * NP)
            project(1, B - 1)
            pe.wait_ge(post, (B - 1) * POST_OPS + 4)
            transpose_u(B - 1)
            gate_mm(B - 1)
            pe.wait_ge(post, B * POST_OPS)
            pe.wait_ge(in_ffn, 16 * FFN_DMAS)

            def turn(k, src):
                pe.wait_ge(tr_in, k + 1)
                for mt in range(2):
                    mm = pe.transpose(ps_x[:, mt * B:(mt + 1) * B], src[:, 128 * mt:128 * mt + 128], ident[0:B, 0:B])
                mm.then_inc(tr8, 1)
                pe.wait_ge(trc8, k + 1)

            def rows(w, n_lin):
                for mt in range(2):
                    mm = pe.matmul(ps_o[0:B, 0:DM], tt[:, mt, :], w[:, mt, :], start=(mt == 0), stop=(mt == 1))
                mm.then_inc(lin8, 1)

            turn(0, w8)
            rows(aggs, 0)
            for k in range(K_STEPS):
                turn(k + 1, w8)
                for hb in range(HID // 128):
                    for mt in range(2):
                        mm = pe.matmul(ps_s[:, 0, hb * B:(hb + 1) * B], d1s[:, mt, 128 * hb:128 * hb + 128], tt[:, mt, :],
                                       start=(mt == 0), stop=(mt == 1))
                mm.then_inc(lin8, 1)
                pe.wait_ge(gelu8, k + 1)
                for hb in range(HID // 128):
                    mm = pe.matmul(ps_o[0:B, 0:DM], ht[:, hb, :], d2s[:, hb, :], start=(hb == 0), stop=(hb == HID // 128 - 1))
                mm.then_inc(lin8, 1)
            turn(K_STEPS + 1, th)
            rows(bcs, 0)
            pe.wait_ge(tr_in, K_STEPS + 3)
            for b in range(B):
                if b >= 2:
                    pe.wait_ge(mixed, b - 1)
                pe.matmul(ps_s[:, b % 2, 0:DM], sels[:, b, :], v8[:, :], start=True, stop=True).then_inc(spread, 1)

        @block.vector
        def _(dve):
            dve.memset(raw_n[:, KT - 1, :], 0.0).then_inc(const_done, 1)
            for i in range(2):
                dve.memset(k_lo[i][64:96, :], 0.0).then_inc(const_done, 1)
            for i in range(4):
                pad = dve.memset(qq[i][64:96, 1, :], 0.0)
            pad.then_inc(const_done, 1)
            dve.memset(pr_last[64:128, :], 0.0).then_inc(const_done, 1)
            dve.wait_ge(const_done, 5)
            for i in range(2):
                dve.memset(k_lo[i][64:65, :], SC).then_inc(const_done, 1)
            dve.memset(ones[:, :], 1.0).then_inc(dve_const, 1)
            for i in range(2):
                dve.wait_ge(wfold, 3 + i)
                dve.tensor_copy(a2[:, 8 * i:8 * i + 8, :].rearrange("p h d -> p (h d)"),
                                ps_m[0:DCQ - 128, 1, 512 * i:512 * i + 512]).then_inc(wcopy, 1)
            dve.wait_ge(in_wa, 48)
            dve.tensor_copy(identb[:, :], ident[:, :]).then_inc(dve_const, 1)
            dve.wait_ge(in_x, 16)
            xv = xs[:, :].rearrange("p (b s m) -> p b s m", b=B, s=ST)
            for b in range(B):
                o = b * LN_OPS
                for st in range(ST):
                    dve.bn_stats(stats[:, st, :], xv[:, b, st, :]).then_inc(ln, 1)
                dve.wait_ge(ln, o + 2)
                for st in range(ST):
                    dve.bn_aggr(mv[:, st, :], stats[:, st, :]).then_inc(ln, 1)
                dve.wait_ge(ln, o + 4)
                dve.tensor_scalar(ve[:, :], mv[:, :, 1], 1e-5, None, ALU.add).then_inc(ln, 1)
                dve.wait_ge(ln_sd, b + 1)
                dve.reciprocal(rs[:, :], sd[:, :]).then_inc(ln, 1)
                dve.wait_ge(ln, o + 6)
                if b >= 2:
                    dve.wait_ge(xt_done, b - 1)
                for st in range(ST):
                    dve.tensor_scalar(xn[b % 2][:, st, :], xv[:, b, st, :], mv[:, st, 0:1], rs[:, st:st + 1],
                                      ALU.subtract, ALU.mult).then_inc(ln, 1)

            def low_part(p, g):
                dve.wait_ge(qh_done, g + 1)
                dve.scalar_tensor_tensor(q_lo[p % 2][:, :], ps_x[:, 0:S], SC, q_hi[p % 2][:, :], ALU.mult,
                                         ALU.subtract).then_inc(ql_done, 1)

            def max_half(g8, i):
                dve.wait_ge(mx_done, g8 + i + 1)
                dve.tensor_reduce(mx[:, i:i + 1], ps_m[:, i % 2, 0:HALF[i % 2]], AX.X, ALU.max).then_inc(mx_read, 1)

            def negate_max(g):
                dve.wait_ge(mx_read, g * 8 + 8)
                if not (isinstance(g, int) and g == 0):
                    dve.wait_ge(mrow_done, g)
                with nc.allow_low_precision("a shift that cancels in the softmax"):
                    dve.tensor_reduce(negm[:, :], mx[:, :].rearrange("p (i h) -> p i h", h=2), AX.X, ALU.max,
                                      negate=True).then_inc(negm_done, 1)

            def add_tile(p, g, t):
                f = POOL_TILES
                if t == f + 1:
                    if not (isinstance(g, int) and g == 0):
                        dve.wait_ge(total_done, g)
                else:
                    dve.wait_ge(sum_d, g * DVE_OPS + (t - f - 1))
                dve.wait_ge(p_done, g * KT + (t + 1))
                r = 128 if t < KT - 1 else LAST
                a = probs(f) if t == f + 1 else acc_d[:, :]
                dve.tensor_tensor(acc_d[0:r, :], a[0:r, :], probs(t)[0:r, :], ALU.add).then_inc(sum_d, 1)

            def join_sums(p, g):
                dve.wait_ge(sum_d, g * DVE_OPS + (DVE_OPS - 1))
                dve.wait_ge(sum_p, g * POOL_OPS + POOL_OPS)
                dve.tensor_tensor(acc_d[:, :], acc_d[:, :], acc_p[p % 2][:, :], ALU.add).then_inc(sum_d, 1)

            def invert(g):
                dve.wait_ge(total_done, g + 1)
                dve.reciprocal(rinv[:, :], ps_x[:, 0:S]).then_inc(rinv_done, 1)

            def normalise(par, p, g):
                dve.wait_ge(rinv_done, g + 1)
                dve.wait_ge(pv_done, g * KT + KT)
                dve.tensor_tensor(ctx_n[par][:, p, :], ps_o[:, 0:S], rinv[:, :], ALU.mult).then_inc(ctx_done, 1)

            def post_a(m):
                o = m * POST_OPS
                c = bass.ds(m * (ST * DM), ST * DM)
                dve.wait_ge(proj_done, m + 1)
                dve.wait_ge(st_done, m * (NP * KT) + NP * KT)
                dve.tensor_tensor(u[:, :, :].rearrange("p s m -> p (s m)"), xs[:, c], ps_x[:, :], ALU.add).then_inc(post, 1)
                dve.wait_ge(post, o + 1)
                for st in range(ST):
                    dve.bn_stats(stats[:, st, :], u[:, st, :]).then_inc(post, 1)
                dve.wait_ge(post, o + 3)
                dve.tensor_tensor(xs[:, c], xs[:, c], ps_x[:, :], ALU.add).then_inc(post, 1)
                for st in range(ST):
                    dve.bn_aggr(mv[:, st, :], stats[:, st, :]).then_inc(post, 1)
                dve.wait_ge(post, o + 6)
                dve.tensor_scalar(ve[:, :], mv[:, :, 1], 1e-5, None, ALU.add).then_inc(post, 1)

            def post_b(m):
                o = m * POST_OPS
                dve.wait_ge(sd_done, m + 1)
                dve.reciprocal(rs[:, :], sd[:, :]).then_inc(post, 1)
                dve.wait_ge(post, o + 8)
                for st in range(ST):
                    dve.tensor_scalar(u[:, st, :], u[:, st, :], mv[:, st, 0:1], rs[:, st:st + 1],
                                      ALU.subtract, ALU.mult).then_inc(post, 1)
                dve.tensor_copy(mean_all[:, bass.ds(m * ST, ST)], mv[:, :, 0]).then_inc(post, 1)
                dve.tensor_copy(rs_all[:, bass.ds(m * ST, ST)], rs[:, :]).then_inc(post, 1)

            def post_c(m):
                dve.wait_ge(gate_done, m + 1)
                dve.wait_ge(in_gate, 32)
                dve.tensor_tensor(z[:, :, :], ps_x[:, :].rearrange("p (s m) -> p s m", s=ST),
                                  gb[:, :].unsqueeze(1).to_broadcast([128, ST, DM]), ALU.add).then_inc(post, 1)

            low_part(0, 0)
            low_part(1, 1)
            for i in range(8):
                max_half(0, i)
            negate_max(0)

            def batch(n, par):
                for p in range(NP):
                    g = n * NP + p
                    started = not (first(n) and p == 0)
                    ahead = not (last(n) and p == NP - 1)
                    for t in range(KT):
                        if t == 0 and started:
                            add_tile(p - 1, g - 1, KT - 1)
                            join_sums(p - 1, g - 1)
                        if t == 3 and started:
                            invert(g - 1)
                        if t == 5 and started:
                            normalise(par if p else 1 - par, (p - 1) % NP, g - 1)
                        if t < 8 and ahead:
                            max_half(g * 8 + 8, t)
                        if t == 7 and not (last(n) and p >= NP - 2):
                            dve.wait_ge(in_qq[p % 2], n * (96 * 4) + 96 * (p // 2 + 1))
                            low_part(p, g + 2)
                        if t == 8 and ahead:
                            negate_max(g + 1)
                        if t > POOL_TILES + 1:
                            add_tile(p, g, t - 1)
                        if not first(n):
                            if p == 2 and t == 2:
                                post_a(n - 1)
                            if p == 3 and t == 4:
                                post_b(n - 1)
                            if p == 6 and t == 0:
                                post_c(n - 1)

            batches(dve, batch)
            g = B * NP - 1
            add_tile(NP - 1, g, KT - 1)
            join_sums(NP - 1, g)
            invert(g)
            normalise(1, NP - 1, g)
            post_a(B - 1)
            post_b(B - 1)
            post_c(B - 1)

            done = 0

            def link(ins):
                nonlocal done
                done += 1
                ins.then_inc(t_dve, 1)
                dve.wait_ge(t_dve, done)

            def norm8(k, dst, src, eps, gamma=None, beta=None):
                link(dve.bn_stats(st8[:, :], src[:, :]))
                link(dve.bn_aggr(mv8[:, :], st8[:, :]))
                dve.tensor_scalar(ve8[:, :], mv8[:, 1:2], eps, None, ALU.add).then_inc(var8, 1)
                dve.wait_ge(dev8, k + 1)
                link(dve.reciprocal(rs8[:, :], sd8[:, :]))
                link(dve.tensor_scalar(dst[:, :], src[:, :], mv8[:, 0:1], rs8[:, 0:1], ALU.subtract, ALU.mult))
                if gamma is not None:
                    link(dve.tensor_tensor(dst[:, :], dst[:, :], gamma, ALU.mult))
                    dve.tensor_tensor(dst[:, :], dst[:, :], beta, ALU.add).then_inc(tr_in, 1)

            def turned(k):
                dve.wait_ge(tr8, k + 1)
                dve.tensor_copy(tt[:, :, :].rearrange("p t b -> p (t b)"), ps_x[:, 0:2 * B]).then_inc(trc8, 1)

            dve.wait_ge(in_row, 16)
            dve.wait_ge(in_ffn, 16 * FFN_DMAS)
            norm8(0, v8, th, 1e-5)
            norm8(1, w8, v8, 1e-6, ig8, ib8)
            turned(0)
            dve.wait_ge(lin8, 1)
            link(dve.tensor_tensor(th[:, :], ps_o[0:B, 0:DM], ab8, ALU.add))
            for k in range(K_STEPS):
                norm8(k + 2, w8, th, 1e-6, pg8, pb8)
                turned(k + 1)
                link(dve.tensor_tensor(th[:, :], th[:, :], db8, ALU.add))
                dve.wait_ge(lin8, 2 * k + 2)
                dve.tensor_tensor(hp[:, :, :], ps_s[:, 0, 0:HID // 128 * B].rearrange("p (t b) -> p t b", b=B),
                                  d1bs.unsqueeze(2).to_broadcast([128, HID // 128, B]), ALU.add).then_inc(pre8, 1)
                dve.wait_ge(lin8, 2 * k + 3)
                ins = dve.tensor_tensor(th[:, :], ps_o[0:B, 0:DM], th[:, :], ALU.add)
                if k < K_STEPS - 1:
                    link(ins)
                else:
                    ins.then_inc(tr_in, 1)
            turned(K_STEPS + 1)
            dve.wait_ge(lin8, 2 * K_STEPS + 2)
            dve.tensor_tensor(v8[:, :], ps_o[0:B, 0:DM], bb8, ALU.add).then_inc(tr_in, 1)

            dve.wait_ge(gate_out, B)

            def stats_of(b):
                dve.wait_ge(added, b + 1)
                for i in range(b * ST, (b + 1) * ST):
                    dve.bn_stats(st_f[:, i, :], gates[:, i * DM:(i + 1) * DM]).then_inc(t_dve, 1)

            for b in range(B):
                g3 = gates[:, b * ST * DM:(b + 1) * ST * DM].rearrange("p (s m) -> p s m", s=ST)
                dve.wait_ge(spread, b + 1)
                dve.tensor_tensor(g3, g3, ps_s[:, b % 2, 0:DM].unsqueeze(1).to_broadcast([128, ST, DM]), ALU.mult).then_inc(mixed, 1)
                if b >= 2:
                    stats_of(b - 2)
            stats_of(B - 2)
            stats_of(B - 1)
            done += B * ST
            dve.wait_ge(t_dve, done)
            for i in range(B * ST):
                dve.bn_aggr(mv_f[:, i, :], st_f[:, i, :]).then_inc(t_dve, 1)
            done += B * ST
            dve.wait_ge(t_dve, done)
            dve.tensor_scalar(ve_f[:, :], mv_f[:, :, 1], 1e-6, None, ALU.add).then_inc(var_f, 1)
            dve.wait_ge(dev_f, 1)
            link(dve.reciprocal(rs_f[:, :], sd_f[:, :]))
            dve.scalar_tensor_tensor(nm_f[:, :], mv_f[:, :, 0], -1.0, rs_f[:, :], ALU.mult, ALU.mult).then_inc(coef_f, 1)
            for b in range(B):
                g3 = gates[:, b * ST * DM:(b + 1) * ST * DM].rearrange("p (s m) -> p s m", s=ST)
                dve.wait_ge(normed, ST * (b + 1))
                dve.tensor_tensor(g3, g3, ogs.unsqueeze(1).to_broadcast([128, ST, DM]), ALU.mult).then_inc(scaled, 1)


def _rope_constants():
    f4 = np.float32
    inv = f4(1) / np.power(f4(10000), np.arange(0, DC, 2, dtype=f4) / f4(DC))
    freqs = np.arange(L, dtype=f4)[:, None] * inv[None, :]
    sin = np.repeat(np.sin(freqs), 2, axis=-1)
    cos = np.repeat(np.cos(freqs), 2, axis=-1)
    sin = np.concatenate([-sin[:, :DC // 2], sin[:, DC // 2:]], axis=1)
    return sin, cos


def _by_tile(table):
    padded = np.zeros((LP, DC), np.float32)
    padded[:L] = table
    return np.ascontiguousarray(padded.reshape(KT, 128, DC).transpose(1, 0, 2).reshape(128, KT * DC))


def kernel(**inputs):
    import concourse.bacc as _bacc
    from concourse.bass_utils import run_bass_kernel_spmd as _run

    a = {k: np.asarray(v) for k, v in inputs.items()}
    w = {k.removeprefix("L0_xattn_").removeprefix("L0_ffn_"): v for k, v in a.items()}
    sin, cos = _rope_constants()
    sel = np.repeat(np.eye(B, dtype=np.float32)[:, :, None], 128, axis=2)
    laid = {
        "x": w["x"], "kv": w["ctx_512"], "kvt": w["ctx_512"].transpose(0, 2, 1),
        "cos_t": cos.T, "sin_t": sin.T, "cos_n": _by_tile(cos), "sin_n": _by_tile(sin),
        "ident_in": np.eye(128, dtype=np.float32), "sel_in": sel,
        "wq": w["Wq"], "wkcq_t": w["w_kc_q"].transpose(0, 2, 1), "wkckv": w["w_kc_kv"],
        "wqr_t": w["W_qr"].transpose(0, 2, 1), "wkr_t": w["W_kr"].transpose(0, 2, 1), "wo_t": w["Wo"].T,
    }
    for name in ("in_gamma", "in_beta", "agg_w", "agg_b", "pn_gamma", "pn_beta", "d1_w", "d2_w", "d2_b",
                 "bc_w", "bc_b", "gate_w", "gate_b", "out_gamma", "out_beta"):
        laid[name] = w[name]
    laid["d1_b"] = w["d1_b"].reshape(HID // 128, 128).T
    laid = {k: np.ascontiguousarray(v) for k, v in laid.items()}

    nc = _bacc.Bacc("TRN2", target_bir_lowering=False, num_devices=1)
    args = {k: nc.dram_tensor(f"{k}_dram", v.shape, mybir.dt.from_np(v.dtype), kind="ExternalInput").ap() for k, v in laid.items()}
    out = nc.dram_tensor("out_dram", (B, S, DM), F32, kind="ExternalOutput").ap()
    build_xattn_ffn(nc, out=out, **args)
    r = _run(nc, [{f"{k}_dram": v for k, v in laid.items()}], core_ids=[0])
    return r.results[0]["out_dram"]
```

```python
from contextlib import ExitStack

import numpy as np

import concourse.bass as bass
from concourse import mybir

F32 = mybir.dt.float32
F16 = mybir.dt.float16
BF16 = mybir.dt.bfloat16
ALU = mybir.AluOpType
ACT = mybir.ActivationFunctionType
AX = mybir.AxisListType

B, S, DM = 8, 256, 256
L, DC = 1601, 64
H, DK, DCQ, DR = 16, 128, 192, 64
HID = 1024
HB = HID // 128
K_STEPS = 4
NP = H // 2
QW = 2 * S
KT = 13
TB = NP * KT
LAST = L - 128 * (KT - 1)
LP = 128 * KT
ST = S // 128
XB = ST * DM
SC = 16.0
LAG = 6
MX_OPS = 13
EARLY = 3
LO_D = (2, 5, 8, 10, 12)
LO_P = tuple(t for t in range(KT) if t not in LO_D)
PV_STEPS = {t: (t - LAG,) for t in range(LAG + 2, KT)}
PV_STEPS[LAG + 1] = (0, 1)
KC = 162
ONE, LOW, FACTOR = DC, DC + 1, 2 * DC + 1
OW = 2 * DC + 1
PREP_OPS = 6
RAW_DMAS = 2
QQ_DMAS = 16 * 6
POST_OPS = 13
FFN_DMAS = 15


def build_xattn_ffn(nc, x, kv, cos_n, sin_n, ident_in, sel_in, wq, wkcq_t, wkckv, wqr, wkr_t, wo_t,
                    in_gamma, in_beta, agg_w, agg_b, pn_gamma, pn_beta, d1_w, d1_b, d2_w, d2_b,
                    bc_w, bc_b, gate_w, gate_b, out_gamma, out_beta, out):
    with ExitStack() as ctx:
        def sb(name, shape, dt=F32):
            return ctx.enter_context(nc.sbuf_tensor(name, shape, dt))

        def sem(name):
            return ctx.enter_context(nc.semaphore(name))

        xs = sb("xs", [128, B * XB])
        xnt = sb("xnt", [128, 2 * B * S])
        mw = sb("mw", [128, 2, H * DC])
        nw = sb("nw", [128, NP, DM])
        cosn = sb("cosn", [128, KT, DC])
        sinn = sb("sinn", [128, KT, DC])
        raw = sb("raw", [128, KT, DC])
        rot = sb("rot", [128, KT, DC])
        k3 = [sb(f"k3_{i}", [128, KT, KC], F16) for i in range(2)]
        k_hi = [sb(f"k_hi{i}", [128, LP], F16) for i in range(2)]
        k_lo = [sb(f"k_lo{i}", [96, LP], F16) for i in range(2)]
        qq = [sb(f"qq{i}", [128, 2, QW], F16) for i in range(4)]
        q_hi = [sb(f"q_hi{i}", [128, S], F16) for i in range(2)]
        q_lo = [sb(f"q_lo{i}", [128, S], F16) for i in range(2)]
        big = sb("big", [128, 12 * QW + 2 * NP * S + B * XB])
        pr = big[:, 0:12 * QW].rearrange("p (t q) -> p t q", t=12)
        pr_last = sb("pr_last", [128, QW])
        ctx_n = [big[:, 12 * QW + i * NP * S:12 * QW + (i + 1) * NP * S].rearrange("p (g q) -> p g q", g=NP)
                 for i in range(2)]
        gates = big[:, 12 * QW + 2 * NP * S:]
        plo_all = sb("plo_all", [128, 12 * QW], F16)
        plo_last = sb("plo_last", [128, QW], F16)
        kl_part = sb("kl_part", [128, 2, ST, DC])
        inv = sb("inv", [128, 2, ST])
        ctx_r = sb("ctx_r", [128, ST, 2, DC])
        ctx_m = sb("ctx_m", [128, ST, 2, DC])
        mxs = [sb(f"mx{i}", [128, 16]) for i in range(2)]
        negm = sb("negm", [128, 4], BF16)
        ident = sb("ident", [128, 128])
        identb = sb("identb", [128, 128], BF16)
        identh = sb("identh", [128, 128], F16)
        u = sb("u", [128, ST, DM])
        ut = sb("ut", [128, 2, S])
        z = sb("z", [128, ST, DM])
        gw = sb("gw", [128, 2, DM])
        gb = sb("gb", [128, DM])
        stats = sb("stats", [128, ST, 6])
        mv = sb("mv", [128, ST, 2])
        ve, sd, rs = (sb(k, [128, ST]) for k in ("ve", "sd", "rs"))
        mean_all = sb("mean_all", [128, B * ST])
        rs_all = sb("rs_all", [128, B * ST])
        bw = sb("bw", [128, H, DR])
        xn = [ut, u]
        st_f = sb("st_f", [128, B * ST, 6])
        mv_f = sb("mv_f", [128, B * ST, 2])
        ve_f, sd_f, rs_f, nm_f = (sb(k, [128, B * ST]) for k in ("ve_f", "sd_f", "rs_f", "nm_f"))

        cut = [0, H * DM, H * DM + H * DK, H * DM + 2 * H * DK, 2 * H * DM + 2 * H * DK, 2 * H * DM + 2 * H * DK + H * DC]
        assert cut[-1] <= big.shape[1]
        wqs, wkcq1, wkcq2, wos, wkckvs = (
            big[:, cut[i]:cut[i + 1]].rearrange("p (h c) -> p h c", h=H) for i in range(5))
        plo_w = plo_all[:, :].bitcast(F32)
        wqr1, wqr2 = (plo_w[:, i * H * DR:(i + 1) * H * DR].rearrange("p (h r) -> p h r", h=H) for i in range(2))
        wkrs = plo_w[:, 2 * H * DR:3 * H * DR].rearrange("p (g c) -> p g c", g=NP)
        m1t = nw

        d1s = xnt[:, 0:2 * HID].rearrange("p (t h) -> p t h", t=2)
        d2s = xnt[:, 2 * HID:4 * HID].rearrange("p (t m) -> p t m", t=HB)
        aggs, bcs = sb("aggs", [128, 2, DM]), sb("bcs", [128, 2, DM])
        ogs, obs = sb("ogs", [128, DM]), sb("obs", [128, DM])
        ig8, ib8, pg8, pb8, ab8, db8, bb8 = (sb(k, [B, DM]) for k in ("ig8", "ib8", "pg8", "pb8", "ab8", "db8", "bb8"))
        d1bs = sb("d1bs", [128, HB])
        sels = sb("sels", [B, B, 128])
        u_all = big[:, 0:B * XB]
        th, v8, w8 = (sb(k, [B, DM]) for k in ("th", "v8", "w8"))
        tt = sb("tt", [128, 2, B])
        hp = sb("hp", [128, HB, B])
        ht = sb("ht", [128, HB, B])
        st8, mv8, ve8, sd8, rs8 = sb("st8", [B, 6]), sb("mv8", [B, 2]), sb("ve8", [B, 1]), sb("sd8", [B, 1]), sb("rs8", [B, 1])

        ps_m = ctx.enter_context(nc.psum_tensor("ps_m", [128, 3, 512], F32))
        ps_s = ctx.enter_context(nc.psum_tensor("ps_s", [128, 2, 512], F32))
        ps_o = ctx.enter_context(nc.psum_tensor("ps_o", [128, 2, 512], F32))
        ps_x = ctx.enter_context(nc.psum_tensor("ps_x", [128, 512], F32))
        ps_oh = ps_o[:, :, 0:ST * OW].rearrange("p h (s c) -> p h s c", s=ST)
        ps_xh = ps_x[:, :].bitcast(F16)

        in_x = [sem(f"in_x{i}") for i in range(B // 2)]
        in_small, in_wa, in_wb, in_wc, in_tab, in_raw, in_gate, in_ffn, in_row = (
            sem(s) for s in ("in_small", "in_wa", "in_wb", "in_wc", "in_tab", "in_raw", "in_gate", "in_ffn", "in_row"))
        pads, dve_const = sem("pads"), sem("dve_const")
        fold, fold_copied = sem("fold"), sem("fold_copied")
        ln, ln_dev, xn_done, xt_done, xt_copied = (sem(s) for s in ("ln", "ln_dev", "xn_done", "xt_done", "xt_copied"))
        prep, kt_done, kt_copied = sem("prep"), sem("kt_done"), sem("kt_copied")
        q_done, qh_done, ql_done = sem("q_done"), sem("qh_done"), sem("ql_done")
        in_qq = [sem("in_qq0"), sem("in_qq1")]
        mx_done, mx_read, negm_done = sem("mx_done"), sem("mx_read"), sem("negm_done")
        mrow_done, mrow_copied = sem("mrow_done"), sem("mrow_copied")
        st_done, p_done, lo_d, lo_p, pv_done = (sem(s) for s in ("st_done", "p_done", "lo_d", "lo_p", "pv_done"))
        kl_copied, inv_done, ctx_read, ctx_done = (sem(s) for s in ("kl_copied", "inv_done", "ctx_read", "ctx_done"))
        ct_done, ct_copied = sem("ct_done"), sem("ct_copied")
        proj_done, post, dev_done = sem("proj_done"), sem("post"), sem("dev_done")
        ut_done, ut_copied, gate_done, gate_out = (sem(s) for s in ("ut_done", "ut_copied", "gate_done", "gate_out"))
        t_dve = sem("t_dve")
        var8, dev8, tr_in, tr8, trc8, lin8, pre8, gelu8 = (
            sem(s) for s in ("var8", "dev8", "tr_in", "tr8", "trc8", "lin8", "pre8", "gelu8"))
        u_ready, xb_ready, spread, mixed, added, var_f, dev_f, coef_f, normed, scaled, final, stored = (
            sem(s) for s in ("u_ready", "xb_ready", "spread", "mixed", "added", "var_f", "dev_f", "coef_f", "normed", "scaled",
                             "final", "stored"))

        block = ctx.enter_context(nc.Block())

        def key_cols(t):
            return slice(128 * t, 128 * t + (128 if t < KT - 1 else LAST))

        def probs(t):
            return pr[:, t, :] if t < KT - 1 else pr_last[:, :]

        def probs_hi(t):
            return probs(t).bitcast(BF16)[:, 1::2]

        def probs_lo(t):
            return plo_all[:, t * QW:(t + 1) * QW] if t < KT - 1 else plo_last[:, :]

        def make_low(eng, t, done):
            r = 128 if t < KT - 1 else LAST
            eng.tensor_tensor(probs_lo(t)[0:r, :], probs(t)[0:r, :], probs_hi(t)[0:r, :], ALU.subtract).then_inc(done, 1)

        def batches(eng, batch):
            batch(0, 0)
            with eng.Fori(0, (B - 2) // 2) as i:
                batch(i * 2 + 1, 1)
                batch(i * 2 + 2, 0)
            batch(B - 1, 1)

        def first(n):
            return isinstance(n, int) and n == 0

        def last(n):
            return isinstance(n, int) and n == B - 1

        @block.sync
        def _(sp):
            sp.dma_start(ident[:, :], ident_in).then_inc(in_small, 16)
            xv = xs[:, :].rearrange("p (b s m) -> p b s m", b=B, s=ST)
            for b in range(0, B, 2):
                sp.dma_start(xv[:, b:b + 2], x[b:b + 2].rearrange("b (s p) m -> p b s m", p=128)).then_inc(in_x[b // 2], 16)

            def load_keys(n):
                sp.dma_start(raw[:, 0:KT - 1, :], kv[n, 0:128 * (KT - 1), :].rearrange("(t p) d -> p t d", p=128)).then_inc(in_raw, 16)
                sp.dma_start(raw[0:LAST, KT - 1, :], kv[n, 128 * (KT - 1):L, :]).then_inc(in_raw, 16)

            sp.dma_start(sinn[:, :, :].rearrange("p t d -> p (t d)"), sin_n).then_inc(in_tab, 16)
            sp.dma_start(cosn[:, :, :].rearrange("p t d -> p (t d)"), cos_n).then_inc(in_tab, 16)
            sp.wait_ge(pads, 1)
            load_keys(0)
            sp.dma_start(wos, wo_t.rearrange("(h k) m -> k h m", k=DK)).then_inc(in_wc, 16)
            sp.dma_start(wkckvs, wkckv.rearrange("h k d -> k h d")).then_inc(in_wc, 16)

            def move_queries(p, g):
                sp.wait_ge(qh_done, g + 1)
                if not (isinstance(g, int) and g < 4):
                    sp.wait_ge(st_done, g * KT - 3 * KT)
                d, r = qq[p % 4], p % 2
                for h in range(2):
                    for j in range(2):
                        sp.dma_start(d[0:64, j, h * S:(h + 1) * S], q_hi[r][64 * h:64 * h + 64, :]).then_inc(in_qq[r], 16)
                sp.wait_ge(ql_done, g + 1)
                for h in range(2):
                    sp.dma_start(d[64:128, 0, h * S:(h + 1) * S], q_lo[r][64 * h:64 * h + 64, :]).then_inc(in_qq[r], 16)

            move_queries(0, 0)
            move_queries(1, 1)
            sp.dma_start(gw[:, :, :], gate_w.rearrange("(t p) m -> p t m", p=128)).then_inc(in_gate, 16)
            sp.dma_start(gb[:, :], gate_b.partition_broadcast(128)).then_inc(in_gate, 16)
            for dst, src in ((aggs, agg_w), (bcs, bc_w)):
                sp.dma_start(dst[:, :, :], src.rearrange("(t p) m -> p t m", p=128)).then_inc(in_ffn, 16)
            for dst, src in ((ogs, out_gamma), (obs, out_beta)):
                sp.dma_start(dst[:, :], src.partition_broadcast(128)).then_inc(in_ffn, 16)
            for dst, src in ((ig8, in_gamma), (ib8, in_beta), (pg8, pn_gamma), (pb8, pn_beta), (ab8, agg_b), (db8, d2_b), (bb8, bc_b)):
                sp.dma_start(dst[:, :], src.partition_broadcast(B)).then_inc(in_ffn, 16)
            sp.dma_start(d1bs[:, :], d1_b).then_inc(in_ffn, 16)
            sp.dma_start(sels[:, :, :], sel_in).then_inc(in_ffn, 16)

            def batch(n, par):
                if not last(n):
                    sp.wait_ge(prep, (n + 1) * PREP_OPS)
                    load_keys(n + 1)
                for p in range(NP - 2 if last(n) else NP):
                    move_queries((p + 2) % NP, n * NP + p + 2)

            batches(sp, batch)
            sp.wait_ge(q_done, B * NP)
            for dst, src in ((d1s, d1_w), (d2s, d2_w)):
                sp.dma_start(dst, src.rearrange("(t p) m -> p t m", p=128)).then_inc(in_ffn, 16)
            sp.wait_ge(post, (B - 1) * POST_OPS + 4)
            sp.dma_start(th[:, :], xs[127:128, :].rearrange("p (b s m) -> p b s m", b=B, s=ST)[:, :, ST - 1, :]).then_inc(in_row, 16)
            for b in range(B):
                sp.wait_ge(final, b + 1)
                sp.dma_start(out[b].rearrange("(s p) m -> p s m", p=128),
                             gates[:, b * XB:(b + 1) * XB].rearrange("p (s m) -> p s m", s=ST)).then_inc(stored, 16)
            sp.wait_ge(stored, 16 * B)

        @block.gpsimd
        def _(pool):
            def keys(n, par, k):
                if k == 0:
                    pool.wait_ge(in_raw, n * (16 * RAW_DMAS) + 16 * RAW_DMAS)
                    if first(n):
                        pool.wait_ge(in_tab, 32)
                        pool.wait_ge(pads, 13)
                else:
                    pool.wait_ge(prep, n * PREP_OPS + k)
                ops = (
                    (rot[:, :, 0:32], raw[:, :, 32:64], sinn[:, :, 0:32], ALU.mult),
                    (rot[:, :, 32:64], raw[:, :, 0:32], sinn[:, :, 32:64], ALU.mult),
                    (raw[:, :, :], raw[:, :, :], cosn[:, :, :], ALU.mult),
                    (k3[par][:, :, 0:DC], raw[:, :, :], rot[:, :, :], ALU.add),
                    (raw[:, :, :], raw[:, :, :], rot[:, :, :], ALU.add),
                    (k3[par][:, :, LOW:LOW + DC], raw[:, :, :], k3[par][:, :, 0:DC], ALU.subtract),
                )
                pool.tensor_tensor(*ops[k]).then_inc(prep, 1)

            for k in range(PREP_OPS):
                keys(0, 0, k)

            when = {1: (0, 1), 2: (2, 3), 3: (4, 5)}

            def batch(n, par):
                for p in range(NP):
                    for t in LO_P:
                        pool.wait_ge(p_done, n * TB + (p * KT + t + 1))
                        make_low(pool, t, lo_p)
                    if not last(n):
                        for k in when.get(p, ()):
                            keys(n + 1, 1 - par, k)

            batches(pool, batch)
            pool.wait_ge(pv_done, B * TB)
            pool.wait_ge(post, B * POST_OPS)
            for i in range(B * ST):
                pool.tensor_scalar(u_all[:, i * DM:(i + 1) * DM], xs[:, i * DM:(i + 1) * DM], mean_all[:, i:i + 1],
                                   rs_all[:, i:i + 1], ALU.subtract, ALU.mult).then_inc(u_ready, 1)
            pool.wait_ge(u_ready, B * ST)
            pool.wait_ge(in_ffn, 16 * FFN_DMAS)
            pool.wait_ge(in_row, 16)
            for i in range(B * ST):
                c = slice(i * DM, (i + 1) * DM)
                pool.tensor_tensor(xs[:, c], xs[:, c], obs[:, :], ALU.add).then_inc(xb_ready, 1)
            for b in range(B):
                c = slice(b * XB, (b + 1) * XB)
                pool.wait_ge(mixed, b + 1)
                pool.tensor_tensor(gates[:, c], gates[:, c], u_all[:, c], ALU.add).then_inc(added, 1)
            pool.wait_ge(xb_ready, B * ST)
            for b in range(B):
                c = slice(b * XB, (b + 1) * XB)
                pool.wait_ge(scaled, b + 1)
                pool.tensor_tensor(gates[:, c], gates[:, c], xs[:, c], ALU.add).then_inc(final, 1)

        @block.scalar
        def _(act):
            for i, (dst, r) in enumerate(((wkcq1, slice(0, 128)), (wkcq2, slice(128, DCQ)))):
                act.dma_start(dst[0:r.stop - r.start], wkcq_t[:, r, :].rearrange("h q k -> q h k")).then_inc(in_wa, 16)
                act.dma_start((wqr1, wqr2)[i][0:r.stop - r.start], wqr[:, r, :].rearrange("h q r -> q h r")).then_inc(in_wa, 16)
            act.dma_start(wqs, wq.rearrange("(h k) m -> k h m", k=DK)).then_inc(in_wb, 16)
            act.dma_start(wkrs, wkr_t.rearrange("g r c -> r g c")).then_inc(in_wb, 16)

            def copy(out_, in_, **kw):
                return act.activation(out_, in_, ACT.Copy, **kw)

            def flat(ap):
                return ap.rearrange("p a b -> p (a b)")

            act.wait_ge(ln, 3)
            act.activation(sd_f[:, :], ve_f[:, :], ACT.Sqrt).then_inc(ln_dev, 1)
            for b in range(B):
                act.wait_ge(xt_done, b + 1)
                copy(xnt[:, :].rearrange("p (t q) -> p t q", t=2)[:, :, b * S:(b + 1) * S],
                     (ps_x[:, :] if b % 2 else ps_o[:, 0, :]).rearrange("p (t q) -> p t q", t=2)).then_inc(xt_copied, 1)
            for i in range(2):
                act.wait_ge(fold, i + 1)
                copy(flat(bw[:, 8 * i:8 * i + 8, :]), ps_s[:, i, :]).then_inc(fold_copied, 1)
            for i in range(4):
                act.wait_ge(fold, 2 + i + 1)
                copy(flat(m1t[:, 2 * i:2 * i + 2, :]), (ps_m[:, 0, :], ps_m[:, 1, :], ps_m[:, 2, :], ps_o[:, 1, :])[i]).then_inc(fold_copied, 1)
            for i in range(4):
                act.wait_ge(fold, 6 + i + 1)
                copy(mw[:, i // 2, (i % 2) * 512:(i % 2 + 1) * 512],
                     (ps_s[:, 0, :], ps_s[:, 1, :], ps_o[:, 0, :], ps_x[:, :])[i]).then_inc(fold_copied, 1)

            def high_part(p, g):
                act.wait_ge(q_done, g + 1)
                copy(q_hi[p % 2][:, :], ps_x[:, 0:S], scale=SC).then_inc(qh_done, 1)

            def copy_keys(n, par, i):
                act.wait_ge(kt_done, n * 4 + (i + 1))
                c = slice(0, 1024) if i % 2 == 0 else slice(1024, LP)
                d = k_hi[par] if i < 2 else k_lo[par]
                r = 128 if i < 2 else 96
                copy(d[0:r, c], ps_xh[0:r, 0:c.stop - c.start]).then_inc(kt_copied, 1)

            def copy_row(p, g):
                act.wait_ge(mrow_done, g + 1)
                copy(qq[p % 4][64:65, 1, :], ps_x[64:65, :], scale=1.0 / SC).then_inc(mrow_copied, 1)

            def copy_low_keys_part(g):
                act.wait_ge(pv_done, g * KT + KT)
                copy(kl_part[:, :, :, :], ps_oh[:, :, :, LOW:OW]).then_inc(kl_copied, 1)

            def copy_ctx(par, p, g):
                act.wait_ge(ct_done, g + 1)
                copy(ctx_n[par][:, p, :], ps_x[:, 0:S]).then_inc(ct_copied, 1)

            act.wait_ge(pads, 13)
            high_part(0, 0)
            high_part(1, 1)
            for i in range(4):
                copy_keys(0, 0, i)
            for i in range(4):
                act.wait_ge(fold, 10 + i + 1)
                copy(flat(nw[:, 2 * i:2 * i + 2, :]), (ps_s[:, 0, :], ps_s[:, 1, :], ps_o[:, 0, :], ps_o[:, 1, :])[i]).then_inc(fold_copied, 1)
            copy_row(0, 0)

            def batch(n, par):
                for p in range(NP):
                    g = n * NP + p
                    started = not (first(n) and p == 0)
                    for t in range(KT):
                        G = n * TB + (p * KT + t)
                        if t == LAG and started:
                            copy_low_keys_part(g - 1)
                        act.wait_ge(st_done, G + 1)
                        if started:
                            act.wait_ge(pv_done, G + 1 - KT)
                        r = 128 if t < KT - 1 else LAST
                        act.activation(probs(t)[0:r, :], ps_s[0:r, (p * KT + t) % 2, :], ACT.Exp, scale=1.0 / SC).then_inc(p_done, 1)
                        if t == 6 and not last(n) and p in (5, 6):
                            copy_keys(n + 1, 1 - par, p - 4)
                        if t == 3 and not (last(n) and p >= NP - 2):
                            act.wait_ge(in_qq[p % 2], n * (QQ_DMAS * 4) + QQ_DMAS * (p // 2 + 1))
                            high_part(p, g + 2)
                        if t == 8 and started:
                            copy_ctx(par if p else 1 - par, (p - 1) % NP, g - 1)
                        if t == 11 and not (last(n) and p == NP - 1):
                            copy_row(p + 1, g + 1)
                        if t == 12 and not last(n) and p in (4, 6):
                            copy_keys(n + 1, 1 - par, 0 if p == 4 else 3)
                        if not first(n):
                            if p == 2 and t == 4:
                                deviation(n - 1)
                            if p == 3 and t == 12:
                                copy_ut(n - 1)
                            if p == 6 and t == 3:
                                gate(n - 1)

            def deviation(m):
                act.wait_ge(post, m * POST_OPS + 7)
                act.activation(sd[:, :], ve[:, :], ACT.Sqrt).then_inc(dev_done, 1)

            def copy_ut(m):
                act.wait_ge(ut_done, m + 1)
                copy(ut[:, :, :], ps_x[:, :].rearrange("p (t q) -> p t q", t=2)).then_inc(ut_copied, 1)

            def gate(m):
                act.wait_ge(post, m * POST_OPS + 13)
                act.activation(gates[:, bass.ds(m * XB, XB)], z[:, :, :].rearrange("p s m -> p (s m)"),
                               ACT.Tanh, scale=0.5).then_inc(gate_out, 1)

            batches(act, batch)
            copy_low_keys_part(B * NP - 1)
            copy_ctx(1, NP - 1, B * NP - 1)
            deviation(B - 1)
            copy_ut(B - 1)
            gate(B - 1)
            for k in range(2 + K_STEPS):
                act.wait_ge(var8, k + 1)
                act.activation(sd8[:, :], ve8[:, :], ACT.Sqrt).then_inc(dev8, 1)
                if k >= 2:
                    act.wait_ge(pre8, k - 1)
                    act.activation(ht[:, :, :], hp[:, :, :], ACT.Gelu).then_inc(gelu8, 1)
            act.wait_ge(var_f, 1)
            act.activation(sd_f[:, :], ve_f[:, :], ACT.Sqrt).then_inc(dev_f, 1)
            act.wait_ge(coef_f, 1)
            for i in range(B * ST):
                act.activation(gates[:, i * DM:(i + 1) * DM], gates[:, i * DM:(i + 1) * DM], ACT.Identity,
                               bias=nm_f[:, i:i + 1], scale=rs_f[:, i:i + 1]).then_inc(normed, 1)

        @block.tensor
        def _(pe):
            pe.wait_ge(in_small, 16)
            for b in range(B):
                pe.wait_ge(xn_done, ST * (b + 1))
                if b >= 2:
                    pe.wait_ge(xt_copied, b - 1)
                for mt in range(2):
                    for st in range(ST):
                        c = mt * S + st * 128
                        mm = pe.transpose((ps_x[:, c:c + 128] if b % 2 else ps_o[:, 0, c:c + 128]),
                                          xn[b % 2][:, st, 128 * mt:128 * mt + 128], ident[:, :])
                mm.then_inc(xt_done, 1)
            pe.wait_ge(in_wa, 64)
            for h in range(H):
                d = ps_s[:, h // 8, (h % 8) * DR:(h % 8 + 1) * DR]
                pe.matmul(d, wkcq1[:, h, :], wqr1[:, h, :], start=True, stop=False)
                mm = pe.matmul(d, wkcq2[0:64, h, :], wqr2[0:64, h, :], start=False, stop=True)
                if h % 8 == 7:
                    mm.then_inc(fold, 1)
            pe.wait_ge(in_wb, 32)
            pe.wait_ge(fold_copied, 2)
            for p in range(NP):
                bank = (ps_m[:, 0, :], ps_m[:, 1, :], ps_m[:, 2, :], ps_o[:, 1, :])[p // 2]
                for h in range(2):
                    mm = pe.matmul(bank[64 * h:64 * h + 64, (p % 2) * DM:(p % 2 + 1) * DM], bw[:, 2 * p + h, :], wqs[:, 2 * p + h, :],
                                   start=True, stop=True)
                if p % 2:
                    mm.then_inc(fold, 1)
            pe.wait_ge(xt_copied, B)
            pe.wait_ge(fold_copied, 6)
            for mt in range(2):
                for p in range(NP):
                    bank = (ps_s[:, 0, :], ps_s[:, 1, :], ps_o[:, 0, :], ps_x[:, :])[mt * 2 + p // 4]
                    mm = pe.matmul(bank[:, (p % 4) * 128:(p % 4 + 1) * 128], m1t[:, p, 128 * mt:128 * mt + 128], wkrs[:, p, :],
                                   start=True, stop=True)
                    if p % 4 == 3:
                        mm.then_inc(fold, 1)

            def queries(n, p, g):
                for mt in range(2):
                    mm = pe.matmul(ps_x[:, 0:S], mw[:, mt, p * 128:(p + 1) * 128], xnt[:, bass.ds(n * S + mt * B * S, S)],
                                   start=(mt == 0), stop=(mt == 1))
                mm.then_inc(q_done, 1)

            def keys_turned(n, par, i):
                pe.wait_ge(prep, n * PREP_OPS + PREP_OPS)
                for t in range(8) if i % 2 == 0 else range(8, KT):
                    c = (t % 8) * 128
                    if i < 2:
                        pe.transpose(ps_xh[:, c:c + 128], k3[par][:, t, 0:128], identh[:, :])
                        mm = pe.transpose(ps_xh[DC:128, c:c + 128], k3[par][:, t, 0:DC], identh[:, :])
                    else:
                        mm = pe.transpose(ps_xh[0:96, c:c + 128], k3[par][:, t, LOW:LOW + 96], identh[:, :])
                mm.then_inc(kt_done, 1)

            def maxima(par, p, g, j):
                if not (isinstance(g, int) and g == 0 and j < 3):
                    pe.wait_ge(mx_read, g * MX_OPS + (j - 2 if j >= 3 else (0, -2, -1)[j]))
                if j < MX_OPS - 1:
                    a = (j // 3) * 128
                    c = (j % 3) * 512
                    mm = pe.matmul(ps_m[:, j % 3, :], qq[p % 4][:, 0, a:a + 128], k_hi[par][:, c:c + 512], start=True, stop=True)
                else:
                    for i in range(4):
                        mm = pe.matmul(ps_m[:, 0, i * LAST:(i + 1) * LAST], qq[p % 4][:, 0, i * 128:(i + 1) * 128],
                                       k_hi[par][:, L - LAST:L], start=True, stop=True)
                mm.then_inc(mx_done, 1)

            def max_row(g):
                pe.wait_ge(negm_done, g + 1)
                for i in range(4):
                    mm = pe.matmul(ps_x[64:65, i * 128:(i + 1) * 128], negm[:, i:i + 1], identb[:, :], start=True, stop=True)
                mm.then_inc(mrow_done, 1)

            pe.wait_ge(fold_copied, 10)
            pe.wait_ge(dve_const, 2)
            queries(0, 0, 0)
            pe.wait_ge(ql_done, 1)
            queries(0, 1, 1)
            pe.wait_ge(ql_done, 2)
            for i in range(4):
                keys_turned(0, 0, i)
                pe.wait_ge(kt_copied, i + 1)
            pe.wait_ge(in_qq[0], QQ_DMAS)
            pe.wait_ge(in_wc, 32)
            for j in range(MX_OPS):
                maxima(0, 0, 0, j)
                if j < 8:
                    bank = (ps_s[:, 0, :], ps_s[:, 1, :], ps_o[:, 0, :], ps_o[:, 1, :])[j // 2]
                    for h in range(2):
                        mm = pe.matmul(bank[64 * h:64 * h + 64, (j % 2) * DM:(j % 2 + 1) * DM], wkckvs[:, 2 * j + h, :], wos[:, 2 * j + h, :],
                                       start=True, stop=True)
                    if j % 2:
                        mm.then_inc(fold, 1)
            max_row(0)
            pe.wait_ge(in_qq[1], QQ_DMAS)
            for j in range(EARLY):
                maxima(0, 1, 1, j)
            pe.wait_ge(fold_copied, 14)

            def p_kv(n, par, p, t):
                g = n * NP + p
                pe.wait_ge(p_done, g * KT + (t + 1))
                for lo in range(2):
                    if lo and t in LO_D:
                        pe.wait_ge(lo_d, g * len(LO_D) + (LO_D.index(t) + 1))
                    elif lo:
                        pe.wait_ge(lo_p, g * len(LO_P) + (LO_P.index(t) + 1))
                    for q in range(4):
                        lhs = (probs_lo(t) if lo else probs_hi(t))[:, q * 128:(q + 1) * 128]
                        w = DC + 1 if lo else OW
                        o = (q % 2) * OW
                        mm = pe.matmul(ps_o[:, q // 2, o:o + w], lhs, k3[par][:, t, 0:w],
                                       start=(t == 0 and not lo and q % 2 == 0), stop=(t == KT - 1 and lo == 1),
                                       skip_group_check=True)
                mm.then_inc(pv_done, 1)

            def ctx_turned(g):
                pe.wait_ge(ctx_done, g + 1)
                for st in range(ST):
                    mm = pe.transpose(ps_x[:, st * 128:st * 128 + 128], ctx_m[:, st, :, :].rearrange("p h d -> p (h d)"), ident[:, :])
                mm.then_inc(ct_done, 1)

            def project(par, m):
                for st in range(ST):
                    for p in range(NP):
                        mm = pe.matmul(ps_x[:, st * DM:(st + 1) * DM], ctx_n[par][:, p, st * 128:st * 128 + 128], nw[:, p, :],
                                       start=(p == 0), stop=(p == NP - 1))
                mm.then_inc(proj_done, 1)

            def transpose_u(m):
                pe.wait_ge(post, m * POST_OPS + 10)
                for mt in range(2):
                    for st in range(ST):
                        mm = pe.transpose(ps_x[:, mt * S + st * 128:mt * S + st * 128 + 128], u[:, st, 128 * mt:128 * mt + 128],
                                          ident[:, :])
                mm.then_inc(ut_done, 1)

            def gate_mm(m):
                pe.wait_ge(ut_copied, m + 1)
                pe.wait_ge(in_gate, 32)
                for st in range(ST):
                    for mt in range(2):
                        mm = pe.matmul(ps_x[:, st * DM:(st + 1) * DM], ut[:, mt, st * 128:st * 128 + 128], gw[:, mt, :],
                                       start=(mt == 0), stop=(mt == 1))
                mm.then_inc(gate_done, 1)

            def batch(n, par):
                m = n - 1
                free = (mrow_copied, n * NP + 1)

                def take_x(after):
                    nonlocal free
                    pe.wait_ge(*free)
                    free = after

                for p in range(NP):
                    g = n * NP + p
                    started = not (first(n) and p == 0)
                    ahead = not (last(n) and p == NP - 1)
                    for t in range(KT):
                        j = p * KT + t
                        c = key_cols(t)
                        r = c.stop - c.start
                        if t == 0:
                            pe.wait_ge(mrow_copied, g + 1)
                            if p == 0 and not first(n):
                                pe.wait_ge(kt_copied, n * 4 + 4)
                        if not (first(n) and j < 2):
                            pe.wait_ge(p_done, n * TB + (j - 1))
                        pe.matmul(ps_s[0:r, j % 2, :], k_hi[par][:, c], qq[p % 4][:, 0, :], start=True, stop=False)
                        pe.matmul(ps_s[0:r, j % 2, :], k_lo[par][:, c], qq[p % 4][0:96, 1, :], start=False, stop=True).then_inc(st_done, 1)
                        if ahead and t < MX_OPS - EARLY:
                            maxima(par if p < NP - 1 else 1 - par, p + 1, g + 1, t + EARLY)
                        if t >= MX_OPS - EARLY and not (last(n) and p >= NP - 2):
                            if t == MX_OPS - EARLY:
                                pe.wait_ge(in_qq[p % 2], n * (QQ_DMAS * 4) + QQ_DMAS * ((p + 2) // 2 + 1))
                                if p == NP - 2:
                                    pe.wait_ge(kt_copied, n * 4 + 6)
                            maxima(par if p < NP - 2 else 1 - par, p + 2, g + 2, t - (MX_OPS - EARLY))
                        if t == 6 and not last(n) and p in (5, 6):
                            take_x((kt_copied, n * 4 + (4 + p - 3)))
                            keys_turned(n + 1, 1 - par, p - 4)
                        if t == 3 and not (last(n) and p >= NP - 2):
                            take_x((ql_done, g + 3))
                            queries(n if p < NP - 2 else n + 1, (p + 2) % NP, g + 2)
                        if t == 8 and started:
                            take_x((ct_copied, g))
                            ctx_turned(g - 1)
                        if t == 11 and ahead:
                            take_x((mrow_copied, g + 2))
                            max_row(g + 1)
                        if t == 12:
                            if p == 1 and not first(n):
                                take_x((post, m * POST_OPS + 4))
                                project(1 - par, m)
                            elif p == 3 and not first(n):
                                take_x((ut_copied, m + 1))
                                transpose_u(m)
                            elif p == 5 and not first(n):
                                take_x((post, m * POST_OPS + 13))
                                gate_mm(m)
                            elif p in (4, 6) and not last(n):
                                i = 0 if p == 4 else 3
                                take_x((kt_copied, n * 4 + (4 + i + 1)))
                                keys_turned(n + 1, 1 - par, i)
                        if t < LAG:
                            if started:
                                if p:
                                    p_kv(n, par, p - 1, t + KT - LAG)
                                else:
                                    p_kv(n - 1, 1 - par, NP - 1, t + KT - LAG)
                        for tt in PV_STEPS.get(t, ()):
                            if tt == 0 and started:
                                pe.wait_ge(ctx_read, g)
                            p_kv(n, par, p, tt)

            batches(pe, batch)
            g = B * NP - 1
            for t in range(KT - LAG, KT):
                p_kv(B - 1, 1, NP - 1, t)
            ctx_turned(g)
            pe.wait_ge(ct_copied, g + 1)
            project(1, B - 1)
            pe.wait_ge(post, (B - 1) * POST_OPS + 4)
            transpose_u(B - 1)
            gate_mm(B - 1)
            pe.wait_ge(post, B * POST_OPS)
            pe.wait_ge(in_ffn, 16 * FFN_DMAS)

            def turn(k, src):
                pe.wait_ge(tr_in, k + 1)
                for mt in range(2):
                    mm = pe.transpose(ps_x[:, mt * B:(mt + 1) * B], src[:, 128 * mt:128 * mt + 128], ident[0:B, 0:B])
                mm.then_inc(tr8, 1)
                pe.wait_ge(trc8, k + 1)

            def rows(w):
                for mt in range(2):
                    mm = pe.matmul(ps_o[0:B, 0, 0:DM], tt[:, mt, :], w[:, mt, :], start=(mt == 0), stop=(mt == 1))
                mm.then_inc(lin8, 1)

            turn(0, w8)
            rows(aggs)
            for k in range(K_STEPS):
                turn(k + 1, w8)
                for hb in range(HB):
                    for mt in range(2):
                        mm = pe.matmul(ps_s[:, 0, hb * B:(hb + 1) * B], d1s[:, mt, 128 * hb:128 * hb + 128], tt[:, mt, :],
                                       start=(mt == 0), stop=(mt == 1))
                mm.then_inc(lin8, 1)
                pe.wait_ge(gelu8, k + 1)
                for hb in range(HB):
                    mm = pe.matmul(ps_o[0:B, 0, 0:DM], ht[:, hb, :], d2s[:, hb, :], start=(hb == 0), stop=(hb == HB - 1))
                mm.then_inc(lin8, 1)
            turn(K_STEPS + 1, th)
            rows(bcs)
            pe.wait_ge(tr_in, K_STEPS + 3)
            for b in range(B):
                if b >= 2:
                    pe.wait_ge(mixed, b - 1)
                pe.matmul(ps_s[:, b % 2, 0:DM], sels[:, b, :], v8[:, :], start=True, stop=True).then_inc(spread, 1)

        @block.vector
        def _(dve):
            def pad(ap, value, after=0):
                if after:
                    dve.wait_ge(pads, after)
                dve.memset(ap, value).then_inc(pads, 1)

            pad(raw[:, KT - 1, :], 0.0)
            pad(pr_last[64:128, :], 0.0)
            pad(plo_last[64:128, :], 0.0)
            for i in range(2):
                pad(k3[i][:, :, ONE:ONE + 1], 1.0)
                pad(k3[i][:, :, FACTOR:FACTOR + 1], SC)
                pad(k3[i][:, :, FACTOR + 1:KC], 0.0)
            for i in range(4):
                pad(qq[i][64:96, 1, :], 0.0)
            dve.wait_ge(in_small, 16)
            dve.tensor_copy(identb[:, :], ident[:, :]).then_inc(dve_const, 1)
            dve.tensor_copy(identh[:, :], ident[:, :]).then_inc(dve_const, 1)
            for i in range(B * ST):
                if i % 4 == 0:
                    dve.wait_ge(in_x[i // 4], 16)
                st_last = dve.bn_stats(st_f[:, i, :], xs[:, i * DM:(i + 1) * DM])
            st_last.then_inc(ln, 1)
            dve.wait_ge(ln, 1)
            for i in range(B * ST):
                aggregated = dve.bn_aggr(mv_f[:, i, :], st_f[:, i, :])
            aggregated.then_inc(ln, 1)
            dve.wait_ge(ln, 2)
            dve.tensor_scalar(ve_f[:, :], mv_f[:, :, 1], 1e-5, None, ALU.add).then_inc(ln, 1)
            dve.wait_ge(ln_dev, 1)
            dve.reciprocal(rs_f[:, :], sd_f[:, :]).then_inc(ln, 1)
            dve.wait_ge(ln, 4)
            for b in range(B):
                if b >= 2:
                    dve.wait_ge(xt_done, b - 1)
                for st in range(ST):
                    i = b * ST + st
                    dve.tensor_scalar(xn[b % 2][:, st, :], xs[:, i * DM:(i + 1) * DM], mv_f[:, i, 0:1], rs_f[:, i:i + 1],
                                      ALU.subtract, ALU.mult).then_inc(xn_done, 1)

            def low_part(p, g):
                dve.wait_ge(qh_done, g + 1)
                dve.scalar_tensor_tensor(q_lo[p % 2][:, :], ps_x[:, 0:S], SC, q_hi[p % 2][:, :], ALU.mult,
                                         ALU.subtract).then_inc(ql_done, 1)

            def read_maxima(p, g, j):
                mx = mxs[p % 2]
                dve.wait_ge(mx_done, g * MX_OPS + (j + 1))
                if j < MX_OPS - 1:
                    k = (j % 3) * 4 + j // 3
                    o, i = mx[:, k:k + 1], ps_m[:, j % 3, :]
                else:
                    o, i = mx[:, 12:16], ps_m[:, 0, 0:4 * LAST].rearrange("p (i k) -> p i k", i=4)
                dve.tensor_reduce(o, i, AX.X, ALU.max).then_inc(mx_read, 1)

            def negate_max(p, g):
                dve.wait_ge(mx_read, g * MX_OPS + MX_OPS)
                if not (isinstance(g, int) and g == 0):
                    dve.wait_ge(mrow_done, g)
                with nc.allow_low_precision("a shift that cancels in the softmax"):
                    dve.tensor_reduce(negm[:, :], mxs[p % 2][:, :].rearrange("p (k i) -> p i k", k=4), AX.X, ALU.max,
                                      negate=True).then_inc(negm_done, 1)

            def low_probs(g, t):
                dve.wait_ge(p_done, g * KT + (t + 1))
                make_low(dve, t, lo_d)

            def normalise(g):
                dve.wait_ge(kl_copied, g + 1)
                dve.reciprocal(inv[:, :, :], ps_oh[:, :, :, ONE]).then_inc(inv_done, 1)
                dve.tensor_tensor(ctx_r[:, :, :, :].rearrange("p s h d -> p h s d"), ps_oh[:, :, :, 0:DC], kl_part[:, :, :, :],
                                  ALU.add).then_inc(ctx_read, 1)
                dve.wait_ge(inv_done, g + 1)
                dve.wait_ge(ctx_read, g + 1)
                if not (isinstance(g, int) and g == 0):
                    dve.wait_ge(ct_done, g)
                dve.tensor_tensor(ctx_m[:, :, :, :].rearrange("p s h d -> p h s d"), ctx_r[:, :, :, :].rearrange("p s h d -> p h s d"),
                                  inv[:, :, :].unsqueeze(3).to_broadcast([128, 2, ST, DC]), ALU.mult).then_inc(ctx_done, 1)

            def post_a(m):
                o = m * POST_OPS
                c = bass.ds(m * XB, XB)
                dve.wait_ge(proj_done, m + 1)
                dve.wait_ge(st_done, m * TB + TB)
                dve.tensor_tensor(u[:, :, :].rearrange("p s m -> p (s m)"), xs[:, c], ps_x[:, :], ALU.add).then_inc(post, 1)
                dve.wait_ge(post, o + 1)
                for st in range(ST):
                    dve.bn_stats(stats[:, st, :], u[:, st, :]).then_inc(post, 1)
                dve.wait_ge(post, o + 3)
                dve.tensor_tensor(xs[:, c], xs[:, c], ps_x[:, :], ALU.add).then_inc(post, 1)
                for st in range(ST):
                    dve.bn_aggr(mv[:, st, :], stats[:, st, :]).then_inc(post, 1)
                dve.wait_ge(post, o + 6)
                dve.tensor_scalar(ve[:, :], mv[:, :, 1], 1e-5, None, ALU.add).then_inc(post, 1)

            def post_b(m):
                o = m * POST_OPS
                dve.wait_ge(dev_done, m + 1)
                dve.reciprocal(rs[:, :], sd[:, :]).then_inc(post, 1)
                dve.wait_ge(post, o + 8)
                for st in range(ST):
                    dve.tensor_scalar(u[:, st, :], u[:, st, :], mv[:, st, 0:1], rs[:, st:st + 1],
                                      ALU.subtract, ALU.mult).then_inc(post, 1)
                dve.tensor_copy(mean_all[:, bass.ds(m * ST, ST)], mv[:, :, 0]).then_inc(post, 1)
                dve.tensor_copy(rs_all[:, bass.ds(m * ST, ST)], rs[:, :]).then_inc(post, 1)

            def post_c(m):
                dve.wait_ge(gate_done, m + 1)
                dve.wait_ge(in_gate, 32)
                dve.tensor_tensor(z[:, :, :], ps_x[:, :].rearrange("p (s m) -> p s m", s=ST),
                                  gb[:, :].unsqueeze(1).to_broadcast([128, ST, DM]), ALU.add).then_inc(post, 1)

            low_part(0, 0)
            low_part(1, 1)
            for j in range(MX_OPS):
                read_maxima(0, 0, j)
            negate_max(0, 0)
            for j in range(EARLY):
                read_maxima(1, 1, j)

            def batch(n, par):
                for p in range(NP):
                    g = n * NP + p
                    started = not (first(n) and p == 0)
                    ahead = not (last(n) and p == NP - 1)
                    for t in range(KT):
                        if t == LAG and started:
                            normalise(g - 1)
                        if t == MX_OPS - EARLY and ahead:
                            negate_max(p + 1, g + 1)
                        if t < MX_OPS - EARLY and ahead:
                            read_maxima(p + 1, g + 1, t + EARLY)
                        if t >= MX_OPS - EARLY and not (last(n) and p >= NP - 2):
                            read_maxima(p, g + 2, t - (MX_OPS - EARLY))
                        if t == 4 and not (last(n) and p >= NP - 2):
                            dve.wait_ge(in_qq[p % 2], n * (QQ_DMAS * 4) + QQ_DMAS * (p // 2 + 1))
                            low_part(p, g + 2)
                        if t == 0 and started and KT - 1 in LO_D:
                            low_probs(g - 1, KT - 1)
                        if t and t - 1 in LO_D:
                            low_probs(g, t - 1)
                        if not first(n):
                            if p == 2 and t == 1:
                                post_a(n - 1)
                            if p == 3 and t == 4:
                                post_b(n - 1)
                            if p == 6 and t == 0:
                                post_c(n - 1)

            batches(dve, batch)
            g = B * NP - 1
            low_probs(g, KT - 1)
            normalise(g)
            post_a(B - 1)
            post_b(B - 1)
            post_c(B - 1)

            done = 0

            def link(ins):
                nonlocal done
                done += 1
                ins.then_inc(t_dve, 1)
                dve.wait_ge(t_dve, done)

            def norm8(k, dst, src, eps, gamma=None, beta=None):
                link(dve.bn_stats(st8[:, :], src[:, :]))
                link(dve.bn_aggr(mv8[:, :], st8[:, :]))
                dve.tensor_scalar(ve8[:, :], mv8[:, 1:2], eps, None, ALU.add).then_inc(var8, 1)
                dve.wait_ge(dev8, k + 1)
                link(dve.reciprocal(rs8[:, :], sd8[:, :]))
                link(dve.tensor_scalar(dst[:, :], src[:, :], mv8[:, 0:1], rs8[:, 0:1], ALU.subtract, ALU.mult))
                if gamma is not None:
                    link(dve.tensor_tensor(dst[:, :], dst[:, :], gamma, ALU.mult))
                    dve.tensor_tensor(dst[:, :], dst[:, :], beta, ALU.add).then_inc(tr_in, 1)

            def turned(k):
                dve.wait_ge(tr8, k + 1)
                dve.tensor_copy(tt[:, :, :].rearrange("p t b -> p (t b)"), ps_x[:, 0:2 * B]).then_inc(trc8, 1)

            dve.wait_ge(in_row, 16)
            dve.wait_ge(in_ffn, 16 * FFN_DMAS)
            norm8(0, v8, th, 1e-5)
            norm8(1, w8, v8, 1e-6, ig8[:, :], ib8[:, :])
            turned(0)
            dve.wait_ge(lin8, 1)
            link(dve.tensor_tensor(th[:, :], ps_o[0:B, 0, 0:DM], ab8[:, :], ALU.add))
            for k in range(K_STEPS):
                norm8(k + 2, w8, th, 1e-6, pg8[:, :], pb8[:, :])
                turned(k + 1)
                link(dve.tensor_tensor(th[:, :], th[:, :], db8[:, :], ALU.add))
                dve.wait_ge(lin8, 2 * k + 2)
                dve.tensor_tensor(hp[:, :, :], ps_s[:, 0, 0:HB * B].rearrange("p (t b) -> p t b", b=B),
                                  d1bs[:, :].unsqueeze(2).to_broadcast([128, HB, B]), ALU.add).then_inc(pre8, 1)
                dve.wait_ge(lin8, 2 * k + 3)
                ins = dve.tensor_tensor(th[:, :], ps_o[0:B, 0, 0:DM], th[:, :], ALU.add)
                if k < K_STEPS - 1:
                    link(ins)
                else:
                    ins.then_inc(tr_in, 1)
            turned(K_STEPS + 1)
            dve.wait_ge(lin8, 2 * K_STEPS + 2)
            dve.tensor_tensor(v8[:, :], ps_o[0:B, 0, 0:DM], bb8[:, :], ALU.add).then_inc(tr_in, 1)

            dve.wait_ge(gate_out, B)

            def stats_of(b):
                dve.wait_ge(added, b + 1)
                for i in range(b * ST, (b + 1) * ST):
                    dve.bn_stats(st_f[:, i, :], gates[:, i * DM:(i + 1) * DM]).then_inc(t_dve, 1)

            for b in range(B):
                g3 = gates[:, b * XB:(b + 1) * XB].rearrange("p (s m) -> p s m", s=ST)
                dve.wait_ge(spread, b + 1)
                dve.scalar_tensor_tensor(g3, g3, 1.0, ps_s[:, b % 2, 0:DM].unsqueeze(1).to_broadcast([128, ST, DM]), ALU.add,
                                         ALU.mult).then_inc(mixed, 1)
                if b >= 2:
                    stats_of(b - 2)
            stats_of(B - 2)
            stats_of(B - 1)
            done += B * ST
            dve.wait_ge(t_dve, done)
            for i in range(B * ST):
                dve.bn_aggr(mv_f[:, i, :], st_f[:, i, :]).then_inc(t_dve, 1)
            done += B * ST
            dve.wait_ge(t_dve, done)
            dve.tensor_scalar(ve_f[:, :], mv_f[:, :, 1], 1e-6, None, ALU.add).then_inc(var_f, 1)
            dve.wait_ge(dev_f, 1)
            link(dve.reciprocal(rs_f[:, :], sd_f[:, :]))
            dve.scalar_tensor_tensor(nm_f[:, :], mv_f[:, :, 0], -1.0, rs_f[:, :], ALU.mult, ALU.mult).then_inc(coef_f, 1)
            for b in range(B):
                g3 = gates[:, b * XB:(b + 1) * XB].rearrange("p (s m) -> p s m", s=ST)
                dve.wait_ge(normed, ST * (b + 1))
                dve.tensor_tensor(g3, g3, ogs[:, :].unsqueeze(1).to_broadcast([128, ST, DM]), ALU.mult).then_inc(scaled, 1)


def _rope_constants():
    f4 = np.float32
    inv = f4(1) / np.power(f4(10000), np.arange(0, DC, 2, dtype=f4) / f4(DC))
    freqs = np.arange(L, dtype=f4)[:, None] * inv[None, :]
    sin = np.repeat(np.sin(freqs), 2, axis=-1)
    cos = np.repeat(np.cos(freqs), 2, axis=-1)
    sin = np.concatenate([-sin[:, :DC // 2], sin[:, DC // 2:]], axis=1)
    return sin, cos


def _by_tile(table):
    padded = np.zeros((LP, DC), np.float32)
    padded[:L] = table
    return np.ascontiguousarray(padded.reshape(KT, 128, DC).transpose(1, 0, 2).reshape(128, KT * DC))


def kernel(**inputs):
    import concourse.bacc as _bacc
    from concourse.bass_utils import run_bass_kernel_spmd as _run

    a = {k: np.asarray(v) for k, v in inputs.items()}
    w = {k.removeprefix("L0_xattn_").removeprefix("L0_ffn_"): v for k, v in a.items()}
    sin, cos = _rope_constants()
    sel = np.repeat(0.5 * np.eye(B, dtype=np.float32)[:, :, None], 128, axis=2)
    wkr = np.zeros((NP, 2, DR, 2, DC), np.float32)
    for h in range(2):
        wkr[:, h, :, h, :] = w["W_kr"][h::2].transpose(0, 2, 1)
    wkr = wkr.reshape(NP, 2 * DR, 2 * DC)
    laid = {
        "x": w["x"], "kv": w["ctx_512"], "cos_n": _by_tile(cos), "sin_n": _by_tile(sin),
        "ident_in": np.eye(128, dtype=np.float32), "sel_in": sel,
        "wq": w["Wq"], "wkcq_t": w["w_kc_q"].transpose(0, 2, 1), "wkckv": w["w_kc_kv"],
        "wqr": w["W_qr"], "wkr_t": wkr, "wo_t": w["Wo"].T,
    }
    for name in ("in_gamma", "in_beta", "agg_w", "agg_b", "pn_gamma", "pn_beta", "d1_w", "d2_w", "d2_b",
                 "bc_w", "bc_b", "gate_w", "gate_b", "out_gamma", "out_beta"):
        laid[name] = w[name]
    laid["d1_b"] = w["d1_b"].reshape(HB, 128).T
    laid = {k: np.ascontiguousarray(v) for k, v in laid.items()}

    nc = _bacc.Bacc("TRN2", target_bir_lowering=False, num_devices=1)
    args = {k: nc.dram_tensor(f"{k}_dram", v.shape, mybir.dt.from_np(v.dtype), kind="ExternalInput").ap() for k, v in laid.items()}
    out = nc.dram_tensor("out_dram", (B, S, DM), F32, kind="ExternalOutput").ap()
    build_xattn_ffn(nc, out=out, **args)
    r = _run(nc, [{f"{k}_dram": v for k, v in laid.items()}], core_ids=[0])
    return r.results[0]["out_dram"]
```

```python
from contextlib import ExitStack

import numpy as np

import concourse.bass as bass
from concourse import mybir

F32 = mybir.dt.float32
F16 = mybir.dt.float16
I32 = mybir.dt.int32
BF16 = mybir.dt.bfloat16
ALU = mybir.AluOpType
ACT = mybir.ActivationFunctionType
AX = mybir.AxisListType

B, S, DM = 8, 256, 256
L, DC = 1601, 64
H, DK, DCQ, DR = 16, 128, 192, 64
HID = 1024
HB = HID // 128
HR = B * (S // 128) // 2
K_STEPS = 4
NP = H // 2
QW = 2 * S
KT = 13
TB = NP * KT
LAST = L - 128 * (KT - 1)
LP = 128 * KT
ST = S // 128
XB = ST * DM
SW = 256.0
SC = 16.0
SPLIT = ((0, 0), (0, 1), (1, 0))
SPLIT_MT = tuple((mt, w, x) for mt in range(2) for w, x in SPLIT)
LAG = 6
MX_OPS = 13
EARLY = 3
LO_D = (0, 2, 4, 10, 12)
LO_P = tuple(t for t in range(KT) if t not in LO_D)
PV_STEPS = {t: (t - LAG,) for t in range(LAG + 2, KT)}
PV_STEPS[LAG + 1] = (0, 1)
KC = 162
ONE, LOW, FACTOR = DC, DC + 1, 2 * DC + 1
OW = 2 * DC + 1
PREP_OPS = 6
RAW_DMAS = 2
QQ_DMAS = 16 * 6
POST_OPS = 12
ROOT_OPS = 12
ROOT_STEPS = {8: 0, 10: 1, 11: 2, 12: 3}
FFN_DMAS = 13


def build_xattn_ffn(nc, x, kv, kv_last, cos_n, sin_n, ident_in, sel_in, wq, wkcq_t, wkckv, wqr, wkr_t, wo_t,
                    in_gamma, in_beta, agg_w, agg_b, pn_gamma, pn_beta, d1_w, d1_b, d2_w, d2_b,
                    bc_w, bc_b, gate_w, gate_b, out_gamma, out_beta, out):
    with ExitStack() as ctx:
        def sb(name, shape, dt=F32):
            return ctx.enter_context(nc.sbuf_tensor(name, shape, dt))

        def sem(name):
            return ctx.enter_context(nc.semaphore(name))

        xs = sb("xs", [128, B * XB])
        xnt = sb("xnt", [128, 2 * B * S])
        xn_hl = [xnt[:, :].bitcast(F16)[:, i * 2 * B * S:(i + 1) * 2 * B * S] for i in range(2)]
        mw = [sb(f"mw{i}", [128, 2, H * DC], F16) for i in range(2)]
        nw32 = sb("nw32", [128, NP * DM])
        nw = [nw32[:, :].bitcast(F16)[:, i * NP * DM:(i + 1) * NP * DM].rearrange("p (g m) -> p g m", g=NP) for i in range(2)]
        tables = sb("tables", [128, 4 * HID])
        cosn, sinn, raw, rot = (tables[:, i * KT * DC:(i + 1) * KT * DC].rearrange("p (t d) -> p t d", t=KT) for i in range(4))
        k3 = [sb(f"k3_{i}", [128, KT, KC], F16) for i in range(2)]
        k_hi = [sb(f"k_hi{i}", [128, LP], F16) for i in range(2)]
        k_lo = [sb(f"k_lo{i}", [96, LP], F16) for i in range(2)]
        qq = [sb(f"qq{i}", [128, 2, QW], F16) for i in range(4)]
        q_hi = [sb(f"q_hi{i}", [128, S], F16) for i in range(2)]
        q_lo = [sb(f"q_lo{i}", [128, S], F16) for i in range(2)]
        big = sb("big", [128, 12 * QW + 2 * NP * S + B * XB])
        pr = big[:, 0:12 * QW].rearrange("p (t q) -> p t q", t=12)
        pr_last = sb("pr_last", [128, QW])
        ctx_n = [big[:, 12 * QW + i * NP * S:12 * QW + (i + 1) * NP * S].bitcast(F16).rearrange("p (g q) -> p g q", g=NP)
                 for i in range(2)]
        gates = big[:, 12 * QW + 2 * NP * S:]
        plo_all = sb("plo_all", [128, 12 * QW], F16)
        plo_last = sb("plo_last", [128, QW], F16)
        o_copy = sb("o_copy", [128, 2, ST, OW])
        inv = sb("inv", [128, 2, ST])
        ctx_r = sb("ctx_r", [128, ST, 2, DC])
        ctx_m = sb("ctx_m", [128, ST, 2, DC])
        ctx_hl = [sb(f"ctx_hl{i}", [128, ST * 2 * DC], F16) for i in range(2)]
        mxs = [sb(f"mx{i}", [128, 16]) for i in range(2)]
        negm = sb("negm", [128, 4], BF16)
        ident = sb("ident", [128, 128])
        identb = sb("identb", [128, 128], BF16)
        identh = sb("identh", [128, 128], F16)
        u = sb("u", [128, ST, DM])
        ut = sb("ut", [128, 2, S])
        z = sb("z", [128, ST, DM])
        gw = sb("gw", [128, 2, DM])
        gb = sb("gb", [128, DM])
        stats = sb("stats", [128, ST, 6])
        mv = sb("mv", [128, ST, 2])
        ve, hv, sq, rs = (sb(k, [128, ST]) for k in ("ve", "hv", "sq", "rs"))
        mean_all = sb("mean_all", [128, B * ST])
        rs_all = sb("rs_all", [128, B * ST])
        bw = sb("bw", [128, H, DR])
        xn = [ut, u]
        st_f = sb("st_f", [128, B * ST, 6])
        mv_f = sb("mv_f", [128, B * ST, 2])
        ve_f, sd_f, rs_f, nm_f = (sb(k, [128, B * ST]) for k in ("ve_f", "sd_f", "rs_f", "nm_f"))

        cut = [0, H * DM, H * DM + H * DK, H * DM + 2 * H * DK, 2 * H * DM + 2 * H * DK, 2 * H * DM + 2 * H * DK + H * DC]
        assert cut[-1] <= big.shape[1]
        wqs, wkcq1, wkcq2, wos, wkckvs = (
            big[:, cut[i]:cut[i + 1]].rearrange("p (h c) -> p h c", h=H) for i in range(5))
        plo_w = plo_all[:, :].bitcast(F32)
        wqr1, wqr2 = (plo_w[:, i * H * DR:(i + 1) * H * DR].rearrange("p (h r) -> p h r", h=H) for i in range(2))
        wkrs = plo_w[:, 2 * H * DR:3 * H * DR].rearrange("p (g c) -> p g c", g=NP)
        m1t = nw32[:, :].rearrange("p (g m) -> p g m", g=NP)

        dw = [xnt[:, :].bitcast(F16)[:, i * 4 * HID:(i + 1) * 4 * HID] for i in range(2)]
        d1s = [w[:, 0:2 * HID].rearrange("p (t h) -> p t h", t=2) for w in dw]
        d2s = [w[:, 2 * HID:4 * HID].rearrange("p (t m) -> p t m", t=HB) for w in dw]
        aggs, bcs = sb("aggs", [128, 2, DM]), sb("bcs", [128, 2, DM])
        ogs, obs = sb("ogs", [128, DM]), sb("obs", [128, DM])
        ig8, ib8, pg8, pb8, ab8, db8, bb8 = (sb(k, [B, DM]) for k in ("ig8", "ib8", "pg8", "pb8", "ab8", "db8", "bb8"))
        d1bs = sb("d1bs", [128, HB])
        sels = sb("sels", [B, B, 128])
        u_all = big[:, 0:B * XB]
        th, v8, w8 = (sb(k, [B, DM]) for k in ("th", "v8", "w8"))
        tt = sb("tt", [128, 2, B])
        ts = [sb(f"ts{i}", [128, 2, B], F16) for i in range(2)]
        yc = sb("yc", [128, 2, B])
        hp = sb("hp", [128, HB, B])
        ht = sb("ht", [128, HB, B])
        hs = [sb(f"hs{i}", [128, HB, B], F16) for i in range(2)]
        st8, mv8, ve8, sd8, rs8 = sb("st8", [B, 6]), sb("mv8", [B, 2]), sb("ve8", [B, 1]), sb("sd8", [B, 1]), sb("rs8", [B, 1])

        ps_m = ctx.enter_context(nc.psum_tensor("ps_m", [128, 3, 512], F32))
        ps_s = ctx.enter_context(nc.psum_tensor("ps_s", [128, 2, 512], F32))
        ps_o = ctx.enter_context(nc.psum_tensor("ps_o", [128, 2, 512], F32))
        ps_x = ctx.enter_context(nc.psum_tensor("ps_x", [128, 512], F32))
        ps_oh = ps_o[:, :, 0:ST * OW].rearrange("p h (s c) -> p h s c", s=ST)
        ps_xh = ps_x[:, :].bitcast(F16)

        in_x = [sem(f"in_x{i}") for i in range(B // 2)]
        in_small, in_wa, in_wb, in_wc, in_tab, in_raw, in_gate, in_ffn, in_dw, in_row = (
            sem(s) for s in ("in_small", "in_wa", "in_wb", "in_wc", "in_tab", "in_raw", "in_gate", "in_ffn", "in_dw", "in_row"))
        pads, dve_const = sem("pads"), sem("dve_const")
        fold, fold_copied, fold_low = sem("fold"), sem("fold_copied"), sem("fold_low")
        ln, ln_dev, xn_act, xn_dve, xt_done, xt_copied, xt_low = (
            sem(s) for s in ("ln", "ln_dev", "xn_act", "xn_dve", "xt_done", "xt_copied", "xt_low"))
        prep, kt_done, kt_copied = sem("prep"), sem("kt_done"), sem("kt_copied")
        q_done, qh_done, ql_done = sem("q_done"), sem("qh_done"), sem("ql_done")
        in_qq = [sem("in_qq0"), sem("in_qq1")]
        mx_done, mx_read, negm_done = sem("mx_done"), sem("mx_read"), sem("negm_done")
        mrow_done, mrow_copied = sem("mrow_done"), sem("mrow_copied")
        st_done, p_done, lo_d, lo_p, pv_done = (sem(s) for s in ("st_done", "p_done", "lo_d", "lo_p", "pv_done"))
        ctx_read, ctx_sum, inv_done, ctx_norm, ctx_high, ctx_done = (
            sem(s) for s in ("ctx_read", "ctx_sum", "inv_done", "ctx_norm", "ctx_high", "ctx_done"))
        ct_done, ct_copied = sem("ct_done"), sem("ct_copied")
        dw_high, dw_low = sem("dw_high"), sem("dw_low")
        proj_done, post, root = sem("proj_done"), sem("post"), sem("root")
        ut_done, ut_copied, gate_done, gate_out = (sem(s) for s in ("ut_done", "ut_copied", "gate_done", "gate_out"))
        t_dve = sem("t_dve")
        var8, dev8, tr_in, tr8, trc8, lin8, pre8, gelu8, low8, col8, colc8 = (
            sem(s) for s in ("var8", "dev8", "tr_in", "tr8", "trc8", "lin8", "pre8", "gelu8", "low8", "col8", "colc8"))
        u_ready, xb_ready, spread, mixed, var_f, dev_f, coef_f, normed, scaled, stored = (
            sem(s) for s in ("u_ready", "xb_ready", "spread", "mixed", "var_f", "dev_f", "coef_f", "normed", "scaled", "stored"))
        added = [sem("added_p"), sem("added_d")]
        final = [sem("final_p"), sem("final_d")]

        block = ctx.enter_context(nc.Block())

        def key_cols(t):
            return slice(128 * t, 128 * t + (128 if t < KT - 1 else LAST))

        def fold_bank(i):
            return (ps_s[:, 0, :], ps_s[:, 1, :], ps_m[:, 2, :], ps_o[:, 1, :])[i]

        def first_key_bank(i):
            return (ps_o[:, 0, :].bitcast(F16), ps_m[:, 0, :].bitcast(F16), ps_m[:, 1, :].bitcast(F16), ps_xh)[i]

        def probs(t):
            return pr[:, t, :] if t < KT - 1 else pr_last[:, :]

        def probs_hi(t):
            return probs(t).bitcast(BF16)[:, 1::2]

        def probs_lo(t):
            return plo_all[:, t * QW:(t + 1) * QW] if t < KT - 1 else plo_last[:, :]

        def make_low(eng, t, done):
            r = 128 if t < KT - 1 else LAST
            eng.tensor_tensor(probs_lo(t)[0:r, :], probs(t)[0:r, :], probs_hi(t)[0:r, :], ALU.subtract).then_inc(done, 1)

        def batches(eng, batch):
            batch(0, 0)
            with eng.Fori(0, (B - 2) // 2) as i:
                batch(i * 2 + 1, 1)
                batch(i * 2 + 2, 0)
            batch(B - 1, 1)

        def first(n):
            return isinstance(n, int) and n == 0

        def last(n):
            return isinstance(n, int) and n == B - 1

        @block.sync
        def _(sp):
            sp.dma_start(ident[:, :], ident_in).then_inc(in_small, 16)
            sp.dma_start(wkcq2[0:DCQ - 128], wkcq_t[128:DCQ]).then_inc(in_wa, 16)
            sp.dma_start(wqr2[0:DCQ - 128], wqr[128:DCQ]).then_inc(in_wa, 16)
            xv = xs[:, :].rearrange("p (b s m) -> p b s m", b=B, s=ST)
            for b in range(0, B, 2):
                sp.dma_start(xv[:, b:b + 2], x[b:b + 2].rearrange("b (s p) m -> p b s m", p=128)).then_inc(in_x[b // 2], 16)

            def load_keys(n):
                sp.dma_start(raw[:, 0:KT - 1, :], kv[n]).then_inc(in_raw, 16)
                sp.dma_start(raw[0:LAST, KT - 1, :], kv_last[n]).then_inc(in_raw, 16)

            sp.dma_start(sinn[:, :, :].rearrange("p t d -> p (t d)"), sin_n).then_inc(in_tab, 16)
            sp.dma_start(cosn[:, :, :].rearrange("p t d -> p (t d)"), cos_n).then_inc(in_tab, 16)
            sp.wait_ge(pads, 1)
            load_keys(0)
            sp.dma_start(wos, wo_t).then_inc(in_wc, 16)
            sp.dma_start(wkckvs, wkckv).then_inc(in_wc, 16)

            def move_queries(p, g):
                sp.wait_ge(qh_done, g + 1)
                if not (isinstance(g, int) and g < 4):
                    sp.wait_ge(st_done, g * KT - 3 * KT)
                d, r = qq[p % 4], p % 2
                for h in range(2):
                    for j in range(2):
                        sp.dma_start(d[0:64, j, h * S:(h + 1) * S], q_hi[r][64 * h:64 * h + 64, :]).then_inc(in_qq[r], 16)
                sp.wait_ge(ql_done, g + 1)
                for h in range(2):
                    sp.dma_start(d[64:128, 0, h * S:(h + 1) * S], q_lo[r][64 * h:64 * h + 64, :]).then_inc(in_qq[r], 16)

            move_queries(0, 0)
            move_queries(1, 1)
            sp.dma_start(gw[:, :, :], gate_w.rearrange("(t p) m -> p t m", p=128)).then_inc(in_gate, 16)
            sp.dma_start(gb[:, :], gate_b.partition_broadcast(128)).then_inc(in_gate, 16)
            for dst, src in ((aggs, agg_w), (bcs, bc_w)):
                sp.dma_start(dst[:, :, :], src.rearrange("(t p) m -> p t m", p=128)).then_inc(in_ffn, 16)
            for dst, src in ((ogs, out_gamma), (obs, out_beta)):
                sp.dma_start(dst[:, :], src.partition_broadcast(128)).then_inc(in_ffn, 16)
            for dst, src in ((ig8, in_gamma), (ib8, in_beta), (pg8, pn_gamma), (pb8, pn_beta), (ab8, agg_b), (db8, d2_b), (bb8, bc_b)):
                sp.dma_start(dst[:, :], src.partition_broadcast(B)).then_inc(in_ffn, 16)
            sp.dma_start(d1bs[:, :], d1_b).then_inc(in_ffn, 16)
            sp.dma_start(sels[:, :, :], sel_in).then_inc(in_ffn, 16)

            def batch(n, par):
                sp.wait_ge(prep, (n + 1) * PREP_OPS)
                if not last(n):
                    load_keys(n + 1)
                else:
                    for i, (src, w) in enumerate(((d1_w, HID), (d2_w, DM))):
                        sp.dma_start(tables[:, i * 2 * HID:(i + 1) * 2 * HID].rearrange("p (t m) -> p t m", m=w),
                                     src.rearrange("(t p) m -> p t m", p=128)).then_inc(in_dw, 16)
                for p in range(NP - 2 if last(n) else NP):
                    move_queries((p + 2) % NP, n * NP + p + 2)

            batches(sp, batch)
            sp.wait_ge(post, (B - 1) * POST_OPS + 4)
            sp.dma_start(th[:, :], xs[127:128, :].rearrange("p (b s m) -> p b s m", b=B, s=ST)[:, :, ST - 1, :]).then_inc(in_row, 16)
            for b in range(B):
                sp.wait_ge(final[b % 2], b // 2 + 1)
                sp.dma_start(out[b].rearrange("(s p) m -> p s m", p=128),
                             gates[:, b * XB:(b + 1) * XB].rearrange("p (s m) -> p s m", s=ST)).then_inc(stored, 16)
            sp.wait_ge(stored, 16 * B)

        @block.gpsimd
        def _(pool):
            def keys(n, par, k):
                if k == 0:
                    pool.wait_ge(in_raw, n * (16 * RAW_DMAS) + 16 * RAW_DMAS)
                    if first(n):
                        pool.wait_ge(in_tab, 32)
                        pool.wait_ge(pads, 13)
                else:
                    pool.wait_ge(prep, n * PREP_OPS + k)
                ops = (
                    (rot[:, :, 0:32], raw[:, :, 32:64], sinn[:, :, 0:32], ALU.mult),
                    (rot[:, :, 32:64], raw[:, :, 0:32], sinn[:, :, 32:64], ALU.mult),
                    (raw[:, :, :], raw[:, :, :], cosn[:, :, :], ALU.mult),
                    (k3[par][:, :, 0:DC], raw[:, :, :], rot[:, :, :], ALU.add),
                    (raw[:, :, :], raw[:, :, :], rot[:, :, :], ALU.add),
                    (k3[par][:, :, LOW:LOW + DC], raw[:, :, :], k3[par][:, :, 0:DC], ALU.subtract),
                )
                pool.tensor_tensor(*ops[k]).then_inc(prep, 1)

            for k in range(PREP_OPS):
                keys(0, 0, k)

            when = {1: (0, 1), 2: (2, 3), 3: (4, 5)}

            def batch(n, par):
                for p in range(NP):
                    for t in LO_P:
                        pool.wait_ge(p_done, n * TB + (p * KT + t + 1))
                        make_low(pool, t, lo_p)
                    if not last(n):
                        for k in when.get(p, ()):
                            keys(n + 1, 1 - par, k)

            batches(pool, batch)
            pool.wait_ge(pv_done, B * TB)
            pool.wait_ge(post, B * POST_OPS - 1)
            for i in range(B * ST):
                pool.tensor_scalar(u_all[:, i * DM:(i + 1) * DM], xs[:, i * DM:(i + 1) * DM], mean_all[:, i:i + 1],
                                   rs_all[:, i:i + 1], ALU.subtract, ALU.mult).then_inc(u_ready, 1)
            pool.wait_ge(u_ready, B * ST)
            pool.wait_ge(in_ffn, 16 * FFN_DMAS)
            pool.wait_ge(in_row, 16)
            for i in range(B * ST):
                c = slice(i * DM, (i + 1) * DM)
                pool.tensor_tensor(xs[:, c], xs[:, c], obs[:, :], ALU.add).then_inc(xb_ready, 1)
            for b in range(0, B, 2):
                c = slice(b * XB, (b + 1) * XB)
                pool.wait_ge(mixed, b + 1)
                pool.tensor_tensor(gates[:, c], gates[:, c], u_all[:, c], ALU.add).then_inc(added[0], 1)
            pool.wait_ge(xb_ready, B * ST)
            for b in range(0, B, 2):
                c = slice(b * XB, (b + 1) * XB)
                pool.wait_ge(scaled, b + 1)
                pool.tensor_tensor(gates[:, c], gates[:, c], xs[:, c], ALU.add).then_inc(final[0], 1)

        @block.scalar
        def _(act):
            act.dma_start(wkcq1, wkcq_t[0:128]).then_inc(in_wa, 16)
            act.dma_start(wqr1, wqr[0:128]).then_inc(in_wa, 16)
            act.dma_start(wqs, wq).then_inc(in_wb, 16)
            act.dma_start(wkrs, wkr_t).then_inc(in_wb, 16)

            def copy(out_, in_, **kw):
                return act.activation(out_, in_, ACT.Copy, **kw)

            def flat(ap):
                return ap.rearrange("p a b -> p (a b)")

            def copy_bw(i):
                act.wait_ge(fold, i + 1)
                copy(flat(bw[:, 8 * i:8 * i + 8, :]), ps_s[:, i, :]).then_inc(fold_copied, 1)

            def normalise_x(b):
                if b >= 2:
                    act.wait_ge(xt_done, b - 1)
                i = b * ST
                act.activation(xn[b % 2][:, 0, :], xs[:, i * DM:(i + 1) * DM], ACT.Identity,
                               bias=nm_f[:, i:i + 1], scale=rs_f[:, i:i + 1]).then_inc(xn_act, 1)

            copy_bw(0)
            act.wait_ge(ln, 3)
            act.activation(sd_f[:, :], ve_f[:, :], ACT.Sqrt).then_inc(ln_dev, 1)
            act.wait_ge(ln, 5)
            normalise_x(0)
            copy_bw(1)
            for b in range(B):
                if b + 1 < B:
                    normalise_x(b + 1)
                act.wait_ge(xt_done, b + 1)
                copy(xn_hl[0].rearrange("p (t q) -> p t q", t=2)[:, :, b * S:(b + 1) * S],
                     (ps_x[:, :] if b % 2 else ps_o[:, 0, :]).rearrange("p (t q) -> p t q", t=2)).then_inc(xt_copied, 1)
                if b % 2:
                    i = b // 2
                    act.wait_ge(fold, 2 + i + 1)
                    copy(flat(m1t[:, 2 * i:2 * i + 2, :]), (ps_m[:, 0, :], ps_m[:, 1, :], ps_m[:, 2, :], ps_o[:, 1, :])[i]).then_inc(fold_copied, 1)
            for i in range(4):
                act.wait_ge(fold, 6 + i + 1)
                copy(mw[0][:, i // 2, (i % 2) * 512:(i % 2 + 1) * 512], fold_bank(i), scale=SW).then_inc(fold_copied, 1)

            def copy_keys(n, par, i, psum=ps_xh):
                act.wait_ge(kt_done, n * 4 + (i + 1))
                c = slice(0, 1024) if i % 2 == 0 else slice(1024, LP)
                d = k_hi[par] if i < 2 else k_lo[par]
                r = 128 if i < 2 else 96
                copy(d[0:r, c], psum[0:r, 0:c.stop - c.start]).then_inc(kt_copied, 1)

            def high_part(p, g):
                act.wait_ge(q_done, g + 1)
                copy(q_hi[p % 2][:, :], ps_x[:, 0:S], scale=SC / SW).then_inc(qh_done, 1)

            def copy_row(p, g):
                act.wait_ge(mrow_done, g + 1)
                copy(qq[p % 4][64:65, 1, :], ps_x[64:65, :], scale=1.0 / SC).then_inc(mrow_copied, 1)

            def copy_o(g):
                act.wait_ge(pv_done, g * KT + KT)
                if not (isinstance(g, int) and g == 0):
                    act.wait_ge(ctx_norm, g)
                copy(o_copy[:, :, :, :], ps_oh[:, :, :, :]).then_inc(ctx_read, 1)

            def copy_ctx(par, p, g):
                act.wait_ge(ct_done, g + 1)
                copy(ctx_n[par][:, p, :], ps_xh[:, 0:2 * S]).then_inc(ct_copied, 1)

            act.wait_ge(pads, 13)
            high_part(0, 0)
            high_part(1, 1)
            for i in range(4):
                copy_keys(0, 0, i, first_key_bank(i))
            for i in range(4):
                act.wait_ge(fold, 10 + i + 1)
                copy(flat(nw[0][:, 2 * i:2 * i + 2, :]), (ps_s[:, 0, :], ps_s[:, 1, :], ps_o[:, 0, :], ps_o[:, 1, :])[i],
                     scale=SW).then_inc(fold_copied, 1)
            copy_row(0, 0)

            def batch(n, par):
                for p in range(NP):
                    g = n * NP + p
                    started = not (first(n) and p == 0)
                    for t in range(KT):
                        G = n * TB + (p * KT + t)
                        if t == LAG and started:
                            copy_o(g - 1)
                        act.wait_ge(st_done, G + 1)
                        if started:
                            act.wait_ge(pv_done, G + 1 - KT)
                        r = 128 if t < KT - 1 else LAST
                        act.activation(probs(t)[0:r, :], ps_s[0:r, (p * KT + t) % 2, :], ACT.Exp, scale=1.0 / SC).then_inc(p_done, 1)
                        if t == 6 and not last(n) and p in (5, 6):
                            copy_keys(n + 1, 1 - par, p - 4)
                        if t == 3 and not (last(n) and p >= NP - 2):
                            act.wait_ge(in_qq[p % 2], n * (QQ_DMAS * 4) + QQ_DMAS * (p // 2 + 1))
                            high_part(p, g + 2)
                        if t == 10 and started:
                            copy_ctx(par if p else 1 - par, (p - 1) % NP, g - 1)
                        if t == 11 and not (last(n) and p == NP - 1):
                            copy_row(p + 1, g + 1)
                        if t == 12 and not last(n) and p in (4, 6):
                            copy_keys(n + 1, 1 - par, 0 if p == 4 else 3)
                        if last(n) and p == NP - 1 and t < 8:
                            if t == 0:
                                act.wait_ge(in_dw, 32)
                                act.wait_ge(q_done, B * NP)
                            copy(dw[0][:, t * 512:(t + 1) * 512], tables[:, t * 512:(t + 1) * 512], scale=SW).then_inc(dw_high, 1)
                        if not first(n):
                            if p == 3 and t == 12:
                                copy_ut(n - 1)
                            if p == 6 and t == 3:
                                gate(n - 1)

            def copy_ut(m, psum=ps_x[:, :]):
                act.wait_ge(ut_done, m + 1)
                copy(ut[:, :, :], psum.rearrange("p (t q) -> p t q", t=2)).then_inc(ut_copied, 1)

            def gate(m):
                act.wait_ge(post, m * POST_OPS + 12)
                act.activation(gates[:, bass.ds(m * XB, XB)], z[:, :, :].rearrange("p s m -> p (s m)"),
                               ACT.Tanh, scale=0.5).then_inc(gate_out, 1)

            batches(act, batch)
            copy_o(B * NP - 1)
            copy_ctx(1, NP - 1, B * NP - 1)
            for k in range(2 + K_STEPS):
                act.wait_ge(var8, k + 1)
                act.activation(sd8[:, :], ve8[:, :], ACT.Sqrt).then_inc(dev8, 1)
                if k >= 2:
                    act.wait_ge(pre8, k - 1)
                    for dst in (ht, hs[0]):
                        act.activation(dst[:, :, :], hp[:, :, :], ACT.Gelu).then_inc(gelu8, 1)
                if k == 2:
                    copy_ut(B - 1, ps_m[:, 0, :])
                if k == 4:
                    gate(B - 1)
            for half in range(2):
                rows_of = slice(half * HR, (half + 1) * HR)
                act.wait_ge(var_f, half + 1)
                act.activation(sd_f[:, rows_of], ve_f[:, rows_of], ACT.Sqrt).then_inc(dev_f, 1)
                act.wait_ge(coef_f, half + 1)
                for i in range(half * HR, (half + 1) * HR):
                    act.activation(gates[:, i * DM:(i + 1) * DM], gates[:, i * DM:(i + 1) * DM], ACT.Identity,
                                   bias=nm_f[:, i:i + 1], scale=rs_f[:, i:i + 1]).then_inc(normed, 1)

        @block.tensor
        def _(pe):
            def keys_turned(n, par, i, psum=ps_xh):
                pe.wait_ge(prep, n * PREP_OPS + PREP_OPS)
                for t in range(8) if i % 2 == 0 else range(8, KT):
                    c = (t % 8) * 128
                    if i < 2:
                        pe.transpose(psum[:, c:c + 128], k3[par][:, t, 0:128], identh[:, :])
                        mm = pe.transpose(psum[DC:128, c:c + 128], k3[par][:, t, 0:DC], identh[:, :])
                    else:
                        mm = pe.transpose(psum[0:96, c:c + 128], k3[par][:, t, LOW:LOW + 96], identh[:, :])
                mm.then_inc(kt_done, 1)

            pe.wait_ge(in_wa, 64)
            for h in range(H):
                d = ps_s[:, h // 8, (h % 8) * DR:(h % 8 + 1) * DR]
                pe.matmul(d, wkcq1[:, h, :], wqr1[:, h, :], start=True, stop=False)
                mm = pe.matmul(d, wkcq2[0:64, h, :], wqr2[0:64, h, :], start=False, stop=True)
                if h % 8 == 7:
                    mm.then_inc(fold, 1)
            pe.wait_ge(in_small, 16)
            for b in range(B):
                pe.wait_ge(xn_act, b + 1)
                pe.wait_ge(xn_dve, b + 1)
                if b >= 2:
                    pe.wait_ge(xt_low, b - 1)
                for mt in range(2):
                    for st in range(ST):
                        c = mt * S + st * 128
                        mm = pe.transpose((ps_x[:, c:c + 128] if b % 2 else ps_o[:, 0, c:c + 128]),
                                          xn[b % 2][:, st, 128 * mt:128 * mt + 128], ident[:, :])
                mm.then_inc(xt_done, 1)
                if b == 0:
                    pe.wait_ge(in_wb, 32)
                p = b
                pe.wait_ge(fold_copied, 1 if p < NP // 2 else 2)
                bank = (ps_m[:, 0, :], ps_m[:, 1, :], ps_m[:, 2, :], ps_o[:, 1, :])[p // 2]
                for h in range(2):
                    mm = pe.matmul(bank[64 * h:64 * h + 64, (p % 2) * DM:(p % 2 + 1) * DM], bw[:, 2 * p + h, :], wqs[:, 2 * p + h, :],
                                   start=True, stop=True)
                if p % 2:
                    mm.then_inc(fold, 1)
            pe.wait_ge(xt_low, B - 1)
            pe.wait_ge(fold_copied, 6)
            pe.wait_ge(dve_const, 2)
            for i in range(3):
                keys_turned(0, 0, i, first_key_bank(i))
            for mt in range(2):
                for p in range(NP):
                    mm = pe.matmul(fold_bank(mt * 2 + p // 4)[:, (p % 4) * 128:(p % 4 + 1) * 128], m1t[:, p, 128 * mt:128 * mt + 128],
                                   wkrs[:, p, :], start=True, stop=True)
                    if p % 4 == 3:
                        mm.then_inc(fold, 1)

            def queries(n, p, g):
                for i, (mt, wi, xi) in enumerate(SPLIT_MT):
                    mm = pe.matmul(ps_x[:, 0:S], mw[wi][:, mt, p * 128:(p + 1) * 128], xn_hl[xi][:, bass.ds(n * S + mt * B * S, S)],
                                   start=(i == 0), stop=(i == len(SPLIT_MT) - 1))
                mm.then_inc(q_done, 1)

            def maxima(par, p, g, j):
                if not (isinstance(g, int) and g == 0 and j < 3):
                    pe.wait_ge(mx_read, g * MX_OPS + {0: -3, 1: 0, 2: -1, MX_OPS - 1: MX_OPS - 2}.get(j, j - 2))
                if j < MX_OPS - 1:
                    a = (j // 3) * 128
                    c = (j % 3) * 512
                    mm = pe.matmul(ps_m[:, j % 3, :], qq[p % 4][:, 0, a:a + 128], k_hi[par][:, c:c + 512], start=True, stop=True)
                else:
                    for i in range(4):
                        mm = pe.matmul(ps_m[:, 1, i * LAST:(i + 1) * LAST], qq[p % 4][:, 0, i * 128:(i + 1) * 128],
                                       k_hi[par][:, L - LAST:L], start=True, stop=True)
                mm.then_inc(mx_done, 1)

            def max_row(g):
                pe.wait_ge(negm_done, g + 1)
                for i in range(4):
                    mm = pe.matmul(ps_x[64:65, i * 128:(i + 1) * 128], negm[:, i:i + 1], identb[:, :], start=True, stop=True)
                mm.then_inc(mrow_done, 1)

            pe.wait_ge(fold_low, 4)
            pe.wait_ge(xt_low, B)
            queries(0, 0, 0)
            pe.wait_ge(ql_done, 1)
            queries(0, 1, 1)
            pe.wait_ge(ql_done, 2)
            keys_turned(0, 0, 3)
            pe.wait_ge(kt_copied, 3)
            pe.wait_ge(in_qq[0], QQ_DMAS)
            pe.wait_ge(in_wc, 32)
            for j in range(MX_OPS):
                maxima(0, 0, 0, j)
                if j < 8:
                    bank = (ps_s[:, 0, :], ps_s[:, 1, :], ps_o[:, 0, :], ps_o[:, 1, :])[j // 2]
                    for h in range(2):
                        mm = pe.matmul(bank[64 * h:64 * h + 64, (j % 2) * DM:(j % 2 + 1) * DM], wkckvs[:, 2 * j + h, :], wos[:, 2 * j + h, :],
                                       start=True, stop=True)
                    if j % 2:
                        mm.then_inc(fold, 1)
            pe.wait_ge(kt_copied, 4)
            max_row(0)
            pe.wait_ge(in_qq[1], QQ_DMAS)
            for j in range(EARLY):
                maxima(0, 1, 1, j)
            pe.wait_ge(fold_low, 8)

            def p_kv(n, par, p, t):
                g = n * NP + p
                pe.wait_ge(p_done, g * KT + (t + 1))
                for lo in range(2):
                    if lo and t in LO_D:
                        pe.wait_ge(lo_d, g * len(LO_D) + (LO_D.index(t) + 1))
                    elif lo:
                        pe.wait_ge(lo_p, g * len(LO_P) + (LO_P.index(t) + 1))
                    for q in range(4):
                        lhs = (probs_lo(t) if lo else probs_hi(t))[:, q * 128:(q + 1) * 128]
                        w = DC + 1 if lo else OW
                        o = (q % 2) * OW
                        mm = pe.matmul(ps_o[:, q // 2, o:o + w], lhs, k3[par][:, t, 0:w],
                                       start=(t == 0 and not lo and q % 2 == 0), stop=(t == KT - 1 and lo == 1),
                                       skip_group_check=True)
                mm.then_inc(pv_done, 1)

            def ctx_turned(g):
                pe.wait_ge(ctx_done, g + 1)
                for i in range(2):
                    for st in range(ST):
                        mm = pe.transpose(ps_xh[:, i * S + st * 128:i * S + st * 128 + 128], ctx_hl[i][:, st * 128:st * 128 + 128],
                                          identh[:, :])
                mm.then_inc(ct_done, 1)

            def project(par, sts):
                for st in sts:
                    for p in range(NP):
                        for i, (c, w) in enumerate(SPLIT):
                            mm = pe.matmul(ps_x[:, st * DM:(st + 1) * DM], ctx_n[par][:, p, c * S + st * 128:c * S + st * 128 + 128],
                                           nw[w][:, p, :], start=(p == 0 and i == 0), stop=(p == NP - 1 and i == len(SPLIT) - 1))
                    mm.then_inc(proj_done, 1)

            def project_last(pairs):
                for p in pairs:
                    for st in range(ST):
                        for i, (c, w) in enumerate(SPLIT):
                            mm = pe.matmul(ps_m[:, st, 0:DM], ctx_n[1][:, p, c * S + st * 128:c * S + st * 128 + 128],
                                           nw[w][:, p, :], start=(p == 0 and i == 0), stop=(p == NP - 1 and i == len(SPLIT) - 1))
                        if p == NP - 1:
                            mm.then_inc(proj_done, 1)

            def transpose_u(m, psum=ps_x):
                pe.wait_ge(post, m * POST_OPS + 10)
                for mt in range(2):
                    for st in range(ST):
                        mm = pe.transpose(psum[:, mt * S + st * 128:mt * S + st * 128 + 128], u[:, st, 128 * mt:128 * mt + 128],
                                          ident[:, :])
                mm.then_inc(ut_done, 1)

            def gate_mm(m, psum=ps_x):
                pe.wait_ge(ut_copied, m + 1)
                pe.wait_ge(in_gate, 32)
                for st in range(ST):
                    for mt in range(2):
                        mm = pe.matmul(psum[:, st * DM:(st + 1) * DM], ut[:, mt, st * 128:st * 128 + 128], gw[:, mt, :],
                                       start=(mt == 0), stop=(mt == 1))
                mm.then_inc(gate_done, 1)

            def batch(n, par):
                m = n - 1
                free = (mrow_copied, n * NP + 1)

                def take_x(after):
                    nonlocal free
                    pe.wait_ge(*free)
                    free = after

                for p in range(NP):
                    g = n * NP + p
                    started = not (first(n) and p == 0)
                    ahead = not (last(n) and p == NP - 1)
                    for t in range(KT):
                        j = p * KT + t
                        c = key_cols(t)
                        r = c.stop - c.start
                        if t == 0:
                            pe.wait_ge(mrow_copied, g + 1)
                            if p == 0 and not first(n):
                                pe.wait_ge(kt_copied, n * 4 + 4)
                        if not (first(n) and j < 2):
                            pe.wait_ge(p_done, n * TB + (j - 1))
                        pe.matmul(ps_s[0:r, j % 2, :], k_hi[par][:, c], qq[p % 4][:, 0, :], start=True, stop=False)
                        pe.matmul(ps_s[0:r, j % 2, :], k_lo[par][:, c], qq[p % 4][0:96, 1, :], start=False, stop=True).then_inc(st_done, 1)
                        if ahead and t < KT - EARLY:
                            maxima(par if p < NP - 1 else 1 - par, p + 1, g + 1, t + EARLY)
                        if t >= KT - EARLY and not (last(n) and p >= NP - 2):
                            if t == KT - EARLY:
                                pe.wait_ge(in_qq[p % 2], n * (QQ_DMAS * 4) + QQ_DMAS * ((p + 2) // 2 + 1))
                                if p == NP - 2:
                                    pe.wait_ge(kt_copied, n * 4 + 6)
                            maxima(par if p < NP - 2 else 1 - par, p + 2, g + 2, t - (KT - EARLY))
                        if p == 2 and t == 0 and not first(n):
                            project(1 - par, (1,))
                        if t == 6 and not last(n) and p in (5, 6):
                            take_x((kt_copied, n * 4 + (4 + p - 3)))
                            keys_turned(n + 1, 1 - par, p - 4)
                        if t == 3 and not (last(n) and p >= NP - 2):
                            take_x((ql_done, g + 3))
                            queries(n if p < NP - 2 else n + 1, (p + 2) % NP, g + 2)
                        if t == 10 and started:
                            take_x((ct_copied, g))
                            ctx_turned(g - 1)
                        if t == 11 and ahead:
                            take_x((mrow_copied, g + 2))
                            max_row(g + 1)
                        if t == 12:
                            if p == 1 and not first(n):
                                take_x((post, m * POST_OPS + 1))
                                project(1 - par, (0,))
                            elif p == 3 and not first(n):
                                take_x((ut_copied, m + 1))
                                transpose_u(m)
                            elif p == 5 and not first(n):
                                take_x((post, m * POST_OPS + 12))
                                gate_mm(m)
                            elif p in (4, 6) and not last(n):
                                i = 0 if p == 4 else 3
                                take_x((kt_copied, n * 4 + (4 + i + 1)))
                                keys_turned(n + 1, 1 - par, i)
                        if last(n) and p == NP - 1 and 1 <= t <= NP - 2:
                            if t == 1:
                                pe.wait_ge(mx_read, B * NP * MX_OPS)
                            project_last((t - 1,))
                        if t < LAG:
                            if started:
                                if p:
                                    p_kv(n, par, p - 1, t + KT - LAG)
                                else:
                                    p_kv(n - 1, 1 - par, NP - 1, t + KT - LAG)
                        for behind in PV_STEPS.get(t, ()):
                            if behind == 0 and started:
                                pe.wait_ge(ctx_read, g)
                            p_kv(n, par, p, behind)

            batches(pe, batch)
            g = B * NP - 1
            for t in range(KT - LAG, KT):
                p_kv(B - 1, 1, NP - 1, t)
            project_last((NP - 2,))
            ctx_turned(g)
            pe.wait_ge(ct_copied, g + 1)
            project_last((NP - 1,))
            pe.wait_ge(in_ffn, 16 * FFN_DMAS)

            def turn(k, src):
                pe.wait_ge(tr_in, k + 1)
                for mt in range(2):
                    mm = pe.transpose(ps_x[:, mt * B:(mt + 1) * B], src[:, 128 * mt:128 * mt + 128], ident[0:B, 0:B])
                mm.then_inc(tr8, 1)
                pe.wait_ge(trc8, k + 1)

            def rows(w):
                for mt in range(2):
                    mm = pe.matmul(ps_o[0:B, 0, 0:DM], tt[:, mt, :], w[:, mt, :], start=(mt == 0), stop=(mt == 1))
                mm.then_inc(lin8, 1)

            turn(0, w8)
            rows(aggs)
            pe.wait_ge(dw_low, 8)
            for k in range(K_STEPS):
                turn(k + 1, w8)
                for hb in range(HB):
                    for mt in range(2):
                        for i, (w, x_) in enumerate(SPLIT):
                            mm = pe.matmul(ps_s[:, 0, hb * B:(hb + 1) * B], d1s[w][:, mt, 128 * hb:128 * hb + 128], ts[x_][:, mt, :],
                                           start=(mt == 0 and i == 0), stop=(mt == 1 and i == len(SPLIT) - 1))
                mm.then_inc(lin8, 1)
                pe.wait_ge(low8, k + 1)
                for mt in range(2):
                    for hb in range(HB):
                        for i, (w, x_) in enumerate(SPLIT):
                            mm = pe.matmul(ps_s[:, 1, mt * B:(mt + 1) * B], d2s[w][:, hb, mt * 128:(mt + 1) * 128], hs[x_][:, hb, :],
                                           start=(hb == 0 and i == 0), stop=(hb == HB - 1 and i == len(SPLIT) - 1))
                mm.then_inc(col8, 1)
                pe.wait_ge(colc8, k + 1)
                for mt in range(2):
                    mm = pe.transpose(ps_o[0:B, 0, mt * 128:(mt + 1) * 128], yc[:, mt, :], ident[:, :])
                mm.then_inc(lin8, 1)
                if k == 0:
                    transpose_u(B - 1, ps_m[:, 0, :])
                if k == 1:
                    gate_mm(B - 1, ps_m[:, 1, :])
            turn(K_STEPS + 1, th)
            rows(bcs)
            pe.wait_ge(tr_in, K_STEPS + 3)
            for b in range(B):
                if b >= 2:
                    pe.wait_ge(mixed, b - 1)
                pe.matmul(ps_s[:, b % 2, 0:DM], sels[:, b, :], v8[:, :], start=True, stop=True).then_inc(spread, 1)

        @block.vector
        def _(dve):
            def pad(ap, value, after=0):
                if after:
                    dve.wait_ge(pads, after)
                dve.memset(ap, value).then_inc(pads, 1)

            pad(raw[:, KT - 1, :], 0.0)
            pad(pr_last[64:128, :], 0.0)
            pad(plo_last[64:128, :], 0.0)
            for i in range(2):
                pad(k3[i][:, :, ONE:ONE + 1], 1.0)
                pad(k3[i][:, :, FACTOR:FACTOR + 1], SC)
                pad(k3[i][:, :, FACTOR + 1:KC], 0.0)
            for i in range(4):
                pad(qq[i][64:96, 1, :], 0.0)
            dve.wait_ge(in_small, 16)
            dve.tensor_copy(identb[:, :], ident[:, :]).then_inc(dve_const, 1)
            dve.tensor_copy(identh[:, :], ident[:, :]).then_inc(dve_const, 1)
            for i in range(B * ST):
                if i % 4 == 0:
                    dve.wait_ge(in_x[i // 4], 16)
                st_last = dve.bn_stats(st_f[:, i, :], xs[:, i * DM:(i + 1) * DM])
            st_last.then_inc(ln, 1)
            dve.wait_ge(ln, 1)
            for i in range(B * ST):
                aggregated = dve.bn_aggr(mv_f[:, i, :], st_f[:, i, :])
            aggregated.then_inc(ln, 1)
            dve.wait_ge(ln, 2)
            dve.tensor_scalar(ve_f[:, :], mv_f[:, :, 1], 1e-5, None, ALU.add).then_inc(ln, 1)
            dve.wait_ge(ln_dev, 1)
            dve.reciprocal(rs_f[:, :], sd_f[:, :]).then_inc(ln, 1)
            dve.wait_ge(ln, 4)
            dve.scalar_tensor_tensor(nm_f[:, :], mv_f[:, :, 0], -1.0, rs_f[:, :], ALU.mult, ALU.mult).then_inc(ln, 1)

            def normalise_x(b):
                if b >= 2:
                    dve.wait_ge(xt_done, b - 1)
                i = b * ST + 1
                dve.tensor_scalar(xn[b % 2][:, 1, :], xs[:, i * DM:(i + 1) * DM], mv_f[:, i, 0:1], rs_f[:, i:i + 1],
                                  ALU.subtract, ALU.mult).then_inc(xn_dve, 1)

            normalise_x(0)
            normalise_x(1)
            for b in range(B):
                dve.wait_ge(xt_copied, b + 1)
                cols = slice(b * S, (b + 1) * S)
                hi, lo = (xn_hl[i].rearrange("p (t q) -> p t q", t=2)[:, :, cols] for i in range(2))
                dve.tensor_tensor(lo, (ps_x[:, :] if b % 2 else ps_o[:, 0, :]).rearrange("p (t q) -> p t q", t=2), hi,
                                  ALU.subtract).then_inc(xt_low, 1)
                if b + 2 < B:
                    normalise_x(b + 2)

            def fold_low_part(hi, lo, psum, after):
                dve.wait_ge(fold_copied, after)
                dve.scalar_tensor_tensor(lo, psum, SW, hi, ALU.mult, ALU.subtract).then_inc(fold_low, 1)

            for i in range(4):
                c = slice((i % 2) * 512, (i % 2 + 1) * 512)
                fold_low_part(mw[0][:, i // 2, c], mw[1][:, i // 2, c],
                              fold_bank(i), 6 + i + 1)

            def low_part(p, g):
                dve.wait_ge(qh_done, g + 1)
                dve.scalar_tensor_tensor(q_lo[p % 2][:, :], ps_x[:, 0:S], SC / SW, q_hi[p % 2][:, :], ALU.mult,
                                         ALU.subtract).then_inc(ql_done, 1)

            def read_maxima(p, g, j):
                mx = mxs[p % 2]
                dve.wait_ge(mx_done, g * MX_OPS + (j + 1))
                if j < MX_OPS - 1:
                    k = (j % 3) * 4 + j // 3
                    o, i = mx[:, k:k + 1], ps_m[:, j % 3, :]
                else:
                    o, i = mx[:, 12:16], ps_m[:, 1, 0:4 * LAST].rearrange("p (i k) -> p i k", i=4)
                dve.tensor_reduce(o, i, AX.X, ALU.max).then_inc(mx_read, 1)

            def negate_max(p, g):
                dve.wait_ge(mx_read, g * MX_OPS + MX_OPS)
                if not (isinstance(g, int) and g == 0):
                    dve.wait_ge(mrow_done, g)
                with nc.allow_low_precision("a shift that cancels in the softmax"):
                    dve.tensor_reduce(negm[:, :], mxs[p % 2][:, :].rearrange("p (k i) -> p i k", k=4), AX.X, ALU.max,
                                      negate=True).then_inc(negm_done, 1)

            def low_probs(g, t):
                dve.wait_ge(p_done, g * KT + (t + 1))
                make_low(dve, t, lo_d)

            def normalise(g):
                dve.wait_ge(ctx_read, g + 1)
                dve.tensor_tensor(ctx_r[:, :, :, :].rearrange("p s h d -> p h s d"), o_copy[:, :, :, 0:DC], o_copy[:, :, :, LOW:OW],
                                  ALU.add).then_inc(ctx_sum, 1)
                dve.reciprocal(inv[:, :, :], o_copy[:, :, :, ONE]).then_inc(inv_done, 1)
                dve.wait_ge(ctx_sum, g + 1)
                dve.wait_ge(inv_done, g + 1)
                dve.tensor_tensor(ctx_m[:, :, :, :].rearrange("p s h d -> p h s d"), ctx_r[:, :, :, :].rearrange("p s h d -> p h s d"),
                                  inv[:, :, :].unsqueeze(3).to_broadcast([128, 2, ST, DC]), ALU.mult).then_inc(ctx_norm, 1)
                flat = ctx_m[:, :, :, :].rearrange("p s h d -> p (s h d)")
                if not (isinstance(g, int) and g == 0):
                    dve.wait_ge(ct_done, g)
                dve.wait_ge(ctx_norm, g + 1)
                dve.tensor_copy(ctx_hl[0][:, :], flat).then_inc(ctx_high, 1)
                dve.wait_ge(ctx_high, g + 1)
                dve.tensor_tensor(ctx_hl[1][:, :], flat, ctx_hl[0][:, :], ALU.subtract).then_inc(ctx_done, 1)

            def post_a(m, psum):
                o = m * POST_OPS
                c = bass.ds(m * XB, XB)
                dve.wait_ge(proj_done, m * ST + ST)
                dve.wait_ge(st_done, m * TB + TB)
                dve.scalar_tensor_tensor(u[:, :, :], psum, 1.0 / SW, xs[:, c].rearrange("p (s m) -> p s m", s=ST), ALU.mult,
                                         ALU.add).then_inc(post, 1)
                dve.wait_ge(post, o + 1)
                for st in range(ST):
                    dve.bn_stats(stats[:, st, :], u[:, st, :]).then_inc(post, 1)
                dve.wait_ge(post, o + 3)
                dve.tensor_scalar(xs[:, c], u[:, :, :].rearrange("p s m -> p (s m)"), 1.0, None, ALU.mult).then_inc(post, 1)
                for st in range(ST):
                    dve.bn_aggr(mv[:, st, :], stats[:, st, :]).then_inc(post, 1)
                dve.wait_ge(post, o + 6)
                dve.tensor_scalar(ve[:, :], mv[:, :, 1], 1e-5, None, ALU.add).then_inc(post, 1)

            def post_root(m, k):
                o = m * ROOT_OPS + 3 * k

                def after(i):
                    dve.wait_ge(root, o + i)

                if k == 0:
                    dve.wait_ge(post, m * POST_OPS + 7)
                    dve.tensor_scalar(rs[:, :].bitcast(I32), ve[:, :].bitcast(I32), 1, None, ALU.arith_shift_right).then_inc(root, 1)
                    dve.tensor_scalar(hv[:, :], ve[:, :], -0.5, None, ALU.mult).then_inc(root, 1)
                    after(2)
                    dve.tensor_scalar(rs[:, :].bitcast(I32), rs[:, :].bitcast(I32), -1.0, float(0x5F3759DF), ALU.mult,
                                      ALU.add).then_inc(root, 1)
                else:
                    after(0)
                    dve.tensor_tensor(sq[:, :], rs[:, :], rs[:, :], ALU.mult).then_inc(root, 1)
                    after(1)
                    dve.tensor_tensor(sq[:, :], sq[:, :], hv[:, :], ALU.mult).then_inc(root, 1)
                    after(2)
                    dve.scalar_tensor_tensor(rs[:, :], sq[:, :], 1.5, rs[:, :], ALU.add, ALU.mult).then_inc(root, 1)
                    if k == 3:
                        after(3)
                        dve.tensor_copy(rs_all[:, bass.ds(m * ST, ST)], rs[:, :]).then_inc(post, 1)

            def post_b(m):
                o = m * POST_OPS
                dve.wait_ge(post, o + 8)
                for st in range(ST):
                    dve.tensor_scalar(u[:, st, :], u[:, st, :], mv[:, st, 0:1], rs[:, st:st + 1],
                                      ALU.subtract, ALU.mult).then_inc(post, 1)
                dve.tensor_copy(mean_all[:, bass.ds(m * ST, ST)], mv[:, :, 0]).then_inc(post, 1)

            def post_c(m, psum):
                dve.wait_ge(gate_done, m + 1)
                dve.wait_ge(in_gate, 32)
                dve.tensor_tensor(z[:, :, :], psum.rearrange("p (s m) -> p s m", s=ST),
                                  gb[:, :].unsqueeze(1).to_broadcast([128, ST, DM]), ALU.add).then_inc(post, 1)

            low_part(0, 0)
            low_part(1, 1)
            for j in range(MX_OPS):
                read_maxima(0, 0, j)
                if j < 8 and j % 2:
                    i = j // 2
                    nh, nl = (w[:, 2 * i:2 * i + 2, :].rearrange("p a b -> p (a b)") for w in nw)
                    fold_low_part(nh, nl, (ps_s[:, 0, :], ps_s[:, 1, :], ps_o[:, 0, :], ps_o[:, 1, :])[i], 10 + i + 1)
            negate_max(0, 0)
            for j in range(EARLY):
                read_maxima(1, 1, j)

            def batch(n, par):
                for p in range(NP):
                    g = n * NP + p
                    started = not (first(n) and p == 0)
                    ahead = not (last(n) and p == NP - 1)
                    for t in range(KT):
                        if t == 8 and started:
                            normalise(g - 1)
                        if ahead and t < KT - EARLY:
                            read_maxima(p + 1, g + 1, t + EARLY)
                        if t == KT - EARLY and ahead:
                            negate_max(p + 1, g + 1)
                        if t >= KT - EARLY and not (last(n) and p >= NP - 2):
                            read_maxima(p, g + 2, t - (KT - EARLY))
                        if t == 4 and not (last(n) and p >= NP - 2):
                            dve.wait_ge(in_qq[p % 2], n * (QQ_DMAS * 4) + QQ_DMAS * (p // 2 + 1))
                            low_part(p, g + 2)
                        if t == 0 and started and KT - 1 in LO_D:
                            low_probs(g - 1, KT - 1)
                        if t and t - 1 in LO_D:
                            low_probs(g, t - 1)
                        if last(n) and p == NP - 1 and 1 <= t <= 8:
                            c = slice((t - 1) * 512, t * 512)
                            dve.wait_ge(dw_high, t)
                            dve.scalar_tensor_tensor(dw[1][:, c], tables[:, c], SW, dw[0][:, c], ALU.mult, ALU.subtract).then_inc(dw_low, 1)
                        if not first(n):
                            if p == 2 and t == 1:
                                post_a(n - 1, ps_x[:, :].rearrange("p (s m) -> p s m", s=ST))
                            if p == 2 and t in ROOT_STEPS:
                                post_root(n - 1, ROOT_STEPS[t])
                            if p == 3 and t == 8:
                                post_b(n - 1)
                            if p == 6 and t == 0:
                                post_c(n - 1, ps_x[:, :])

            batches(dve, batch)
            g = B * NP - 1
            low_probs(g, KT - 1)
            normalise(g)
            post_a(B - 1, ps_m[:, 0:ST, 0:DM])

            done = 0

            def link(ins, wait=True):
                nonlocal done
                done += 1
                ins.then_inc(t_dve, 1)
                if wait:
                    dve.wait_ge(t_dve, done)

            def norm8(k, dst, src, eps, gamma=None, beta=None):
                link(dve.bn_stats(st8[:, :], src[:, :]))
                link(dve.bn_aggr(mv8[:, :], st8[:, :]))
                dve.tensor_scalar(ve8[:, :], mv8[:, 1:2], eps, None, ALU.add).then_inc(var8, 1)
                if gamma is None:
                    dve.wait_ge(dev8, k + 1)
                    link(dve.reciprocal(rs8[:, :], sd8[:, :]))
                    link(dve.tensor_scalar(dst[:, :], src[:, :], mv8[:, 0:1], rs8[:, 0:1], ALU.subtract, ALU.mult))
                else:
                    link(dve.scalar_tensor_tensor(dst[:, :], src[:, :], mv8[:, 0:1], gamma, ALU.subtract, ALU.mult))
                    dve.wait_ge(dev8, k + 1)
                    link(dve.reciprocal(rs8[:, :], sd8[:, :]))
                    dve.scalar_tensor_tensor(dst[:, :], dst[:, :], rs8[:, 0:1], beta, ALU.mult, ALU.add).then_inc(tr_in, 1)

            def turned(k):
                dve.wait_ge(tr8, k + 1)
                dve.tensor_copy(tt[:, :, :].rearrange("p t b -> p (t b)"), ps_x[:, 0:2 * B]).then_inc(trc8, 1)

            def turned_parts(k):
                dve.wait_ge(tr8, k + 1)
                hi, lo = (t_[:, :, :].rearrange("p t b -> p (t b)") for t_ in ts)
                link(dve.tensor_copy(hi, ps_x[:, 0:2 * B]))
                dve.tensor_tensor(lo, ps_x[:, 0:2 * B], hi, ALU.subtract).then_inc(trc8, 1)

            dve.wait_ge(in_row, 16)
            dve.wait_ge(in_ffn, 16 * FFN_DMAS)
            norm8(0, v8, th, 1e-5)
            norm8(1, w8, v8, 1e-6, ig8[:, :], ib8[:, :])
            turned(0)
            dve.wait_ge(lin8, 1)
            link(dve.tensor_tensor(th[:, :], ps_o[0:B, 0, 0:DM], ab8[:, :], ALU.add))
            for k in range(K_STEPS):
                norm8(k + 2, w8, th, 1e-6, pg8[:, :], pb8[:, :])
                turned_parts(k + 1)
                link(dve.tensor_tensor(th[:, :], th[:, :], db8[:, :], ALU.add))
                if k == 0:
                    for i in range(4):
                        post_root(B - 1, i)
                    post_b(B - 1)
                if k == 2:
                    post_c(B - 1, ps_m[:, 1, :])
                dve.wait_ge(lin8, 2 * k + 2)
                dve.scalar_tensor_tensor(hp[:, :, :], ps_s[:, 0, 0:HB * B].rearrange("p (t b) -> p t b", b=B), 1.0 / SW,
                                         d1bs[:, :].unsqueeze(2).to_broadcast([128, HB, B]), ALU.mult, ALU.add).then_inc(pre8, 1)
                dve.wait_ge(gelu8, 2 * k + 2)
                dve.tensor_tensor(hs[1][:, :, :], ht[:, :, :], hs[0][:, :, :], ALU.subtract).then_inc(low8, 1)
                dve.wait_ge(col8, k + 1)
                dve.tensor_copy(yc[:, :, :].rearrange("p t b -> p (t b)"), ps_s[:, 1, 0:2 * B]).then_inc(colc8, 1)
                dve.wait_ge(lin8, 2 * k + 3)
                ins = dve.scalar_tensor_tensor(th[:, :], ps_o[0:B, 0, 0:DM], 1.0 / SW, th[:, :], ALU.mult, ALU.add)
                if k < K_STEPS - 1:
                    link(ins)
                else:
                    ins.then_inc(tr_in, 1)
            turned(K_STEPS + 1)
            dve.wait_ge(lin8, 2 * K_STEPS + 2)
            dve.tensor_tensor(v8[:, :], ps_o[0:B, 0, 0:DM], bb8[:, :], ALU.add).then_inc(tr_in, 1)

            dve.wait_ge(gate_out, B)
            dve.wait_ge(u_ready, B * ST)

            def mix(b):
                g3 = gates[:, b * XB:(b + 1) * XB].rearrange("p (s m) -> p s m", s=ST)
                dve.wait_ge(spread, b + 1)
                dve.scalar_tensor_tensor(g3, g3, 1.0, ps_s[:, b % 2, 0:DM].unsqueeze(1).to_broadcast([128, ST, DM]), ALU.add,
                                         ALU.mult).then_inc(mixed, 1)
                if b % 2:
                    c = slice(b * XB, (b + 1) * XB)
                    dve.wait_ge(mixed, b + 1)
                    dve.tensor_tensor(gates[:, c], gates[:, c], u_all[:, c], ALU.add).then_inc(added[1], 1)

            def stats_of(b):
                dve.wait_ge(added[b % 2], b // 2 + 1)
                for i in range(b * ST, (b + 1) * ST):
                    link(dve.bn_stats(st_f[:, i, :], gates[:, i * DM:(i + 1) * DM]), i % ST == ST - 1)

            def variances(half):
                for i in range(half * HR, (half + 1) * HR):
                    link(dve.bn_aggr(mv_f[:, i, :], st_f[:, i, :]), i % HR == HR - 1)
                r = slice(half * HR, (half + 1) * HR)
                dve.tensor_scalar(ve_f[:, r], mv_f[:, r, 1], 1e-6, None, ALU.add).then_inc(var_f, 1)

            def coefficients(half):
                r = slice(half * HR, (half + 1) * HR)
                dve.wait_ge(dev_f, half + 1)
                link(dve.reciprocal(rs_f[:, r], sd_f[:, r]))
                dve.scalar_tensor_tensor(nm_f[:, r], mv_f[:, r, 0], -1.0, rs_f[:, r], ALU.mult, ALU.mult).then_inc(coef_f, 1)

            for half in range(2):
                b0 = half * B // 2
                for b in range(b0, b0 + B // 2):
                    mix(b)
                    if half and b == b0:
                        coefficients(0)
                    if b > b0:
                        stats_of(b - 1)
                stats_of(b0 + B // 2 - 1)
                variances(half)
            for b in range(B):
                if b == 1:
                    coefficients(1)
                c = slice(b * XB, (b + 1) * XB)
                g3 = gates[:, c].rearrange("p (s m) -> p s m", s=ST)
                dve.wait_ge(normed, ST * (b + 1))
                dve.tensor_tensor(g3, g3, ogs[:, :].unsqueeze(1).to_broadcast([128, ST, DM]), ALU.mult).then_inc(scaled, 1)
                if b % 2:
                    dve.wait_ge(scaled, b + 1)
                    dve.wait_ge(xb_ready, B * ST)
                    dve.tensor_tensor(gates[:, c], gates[:, c], xs[:, c], ALU.add).then_inc(final[1], 1)


def _rope_constants():
    f4 = np.float32
    inv = f4(1) / np.power(f4(10000), np.arange(0, DC, 2, dtype=f4) / f4(DC))
    freqs = np.arange(L, dtype=f4)[:, None] * inv[None, :]
    sin = np.repeat(np.sin(freqs), 2, axis=-1)
    cos = np.repeat(np.cos(freqs), 2, axis=-1)
    sin = np.concatenate([-sin[:, :DC // 2], sin[:, DC // 2:]], axis=1)
    return sin, cos


def _by_tile(table):
    padded = np.zeros((LP, DC), np.float32)
    padded[:L] = table
    return np.ascontiguousarray(padded.reshape(KT, 128, DC).transpose(1, 0, 2).reshape(128, KT * DC))


def kernel(**inputs):
    import concourse.bacc as _bacc
    from concourse.bass_utils import run_bass_kernel_spmd as _run

    a = {k: np.asarray(v) for k, v in inputs.items()}
    w = {k.removeprefix("L0_xattn_").removeprefix("L0_ffn_"): v for k, v in a.items()}
    sin, cos = _rope_constants()
    sel = np.repeat(0.5 * np.eye(B, dtype=np.float32)[:, :, None], 128, axis=2)
    wkr = np.zeros((NP, 2, DR, 2, DC), np.float32)
    for h in range(2):
        wkr[:, h, :, h, :] = w["W_kr"][h::2].transpose(0, 2, 1)
    wkr = wkr.reshape(NP, 2 * DR, 2 * DC)
    laid = {
        "x": w["x"], "kv": w["ctx_512"][:, 0:128 * (KT - 1)].reshape(B, KT - 1, 128, DC).transpose(0, 2, 1, 3),
        "kv_last": w["ctx_512"][:, 128 * (KT - 1):], "cos_n": _by_tile(cos), "sin_n": _by_tile(sin),
        "ident_in": np.eye(128, dtype=np.float32), "sel_in": sel,
        "wq": w["Wq"].reshape(H, DK, DM).transpose(1, 0, 2), "wkcq_t": w["w_kc_q"].transpose(2, 0, 1),
        "wkckv": w["w_kc_kv"].transpose(1, 0, 2), "wqr": w["W_qr"].transpose(1, 0, 2),
        "wkr_t": wkr.transpose(1, 0, 2), "wo_t": w["Wo"].T.reshape(H, DK, DM).transpose(1, 0, 2),
    }
    for name in ("in_gamma", "in_beta", "agg_w", "agg_b", "pn_gamma", "pn_beta", "d1_w", "d2_w", "d2_b",
                 "bc_w", "bc_b", "gate_w", "gate_b", "out_gamma", "out_beta"):
        laid[name] = w[name]
    laid["d1_b"] = w["d1_b"].reshape(HB, 128).T
    laid = {k: np.ascontiguousarray(v) for k, v in laid.items()}

    nc = _bacc.Bacc("TRN2", target_bir_lowering=False, num_devices=1)
    args = {k: nc.dram_tensor(f"{k}_dram", v.shape, mybir.dt.from_np(v.dtype), kind="ExternalInput").ap() for k, v in laid.items()}
    out = nc.dram_tensor("out_dram", (B, S, DM), F32, kind="ExternalOutput").ap()
    build_xattn_ffn(nc, out=out, **args)
    r = _run(nc, [{f"{k}_dram": v for k, v in laid.items()}], core_ids=[0])
    return r.results[0]["out_dram"]
```
